# Optimizing a Trainium2 kernel written in Bass

```python
import numpy as np
import jax
import jax.numpy as jnp

def _softmax(x, axis=-1):
    return jax.nn.softmax(x, axis=axis)

def _gelu(x):
    return jax.nn.gelu(x, approximate=True)

def _silu(x):
    return jax.nn.silu(x)

def _sigmoid(x):
    return jax.nn.sigmoid(x)

def _layernorm(x, axis=-1, eps=1e-05):
    m = jnp.mean(x, axis=axis, keepdims=True)
    v = jnp.var(x, axis=axis, keepdims=True)
    return (x - m) / jnp.sqrt(v + eps)

def _scatter_add(tgt, idx, src, axis=0):
    return tgt.at[idx].add(src)

def _segment_sum(src, seg, n):
    return jax.ops.segment_sum(src, seg, n)
kernel_name = 'mk_adj_preln_d2_adj_r2_fb5e5c'

def setup_inputs(seed: int=0):
    np.random.seed(seed)
    _w = jnp.asarray

    def _rec_inputs():
        import jax
        import jax.numpy as jnp
        _gk = jax.random.key(seed)
        x = 7.22e-05 + 1 * jax.random.normal(jax.random.fold_in(_gk, 1), (128, 64, 256), jnp.float32)
        _a = jax.random.bernoulli(jax.random.fold_in(_gk, 2), 0.125, (64, 64))
        _a = jnp.logical_or(_a, jnp.swapaxes(_a, -1, -2))
        _a = jnp.logical_or(_a, jnp.eye(64, dtype=bool))
        _af = _a.astype(jnp.float32)
        adj = _af
        return (x, adj)
    x, adj = _rec_inputs()

    def _L0_gnn_setup():
        import jax, jax.numpy as jnp
        import numpy as np
        B, N, D = (8, 1024, 256)
        key = jax.random.key(seed)
        k1, k2, k3, k4, k5 = jax.random.split(key, 5)
        neuron_states = jax.random.normal(k1, (B, N, D), dtype=jnp.float32)
        adjacency = jax.random.randint(k2, (N, N), 0, 2).astype(jnp.float32)
        scale = 1.0 / np.sqrt(D)
        Wq = jax.random.normal(k3, (D, D), dtype=jnp.float32) * scale
        Wk = jax.random.normal(k4, (D, D), dtype=jnp.float32) * scale
        Wv = jax.random.normal(k5, (D, D), dtype=jnp.float32) * scale
        return {'neuron_states': neuron_states, 'adjacency': adjacency, 'Wq': Wq, 'Wk': Wk, 'Wv': Wv}
    _L0_gnn_all = _L0_gnn_setup()
    _L0_gnn_in = {k: v for k, v in _L0_gnn_all.items() if k in ('Wq', 'Wk', 'Wv')}
    del _L0_gnn_all

    def _L1_gnn_setup():
        import jax, jax.numpy as jnp
        import numpy as np
        B, N, D, T = (64, 128, 256, 3)

        def _lin(v, W, b):
            return jnp.einsum('...i,oi->...o', v, W) + b
        key = jax.random.key(seed)
        ks = jax.random.split(key, 12)
        s2 = 1.0 / np.sqrt(2 * D)
        s1 = 1.0 / np.sqrt(D)
        return {'x': jax.random.normal(ks[0], (B, N, D), jnp.float32), 'in_mat': jax.random.uniform(ks[1], (N, N), jnp.float32) / N, 'out_mat': jax.random.uniform(ks[2], (N, N), jnp.float32) / N, 'w3_w': jax.random.normal(ks[3], (D, 2 * D), jnp.float32) * s2, 'w3_b': jnp.zeros((D,), jnp.float32), 'u3_w': jax.random.normal(ks[4], (D, D), jnp.float32) * s1, 'u3_b': jnp.zeros((D,), jnp.float32), 'w4_w': jax.random.normal(ks[5], (D, 2 * D), jnp.float32) * s2, 'w4_b': jnp.zeros((D,), jnp.float32), 'w5_w': jax.random.normal(ks[6], (D, 2 * D), jnp.float32) * s2, 'w5_b': jnp.zeros((D,), jnp.float32), 'u5_w': jax.random.normal(ks[7], (D, D), jnp.float32) * s1, 'u5_b': jnp.zeros((D,), jnp.float32)}
    _L1_gnn_all = _L1_gnn_setup()
    _L1_gnn_in = {k: v for k, v in _L1_gnn_all.items() if k in ('w3_w', 'w3_b', 'u3_w', 'u3_b', 'w4_w', 'w4_b', 'w5_w', 'w5_b', 'u5_w', 'u5_b')}
    del _L1_gnn_all
    return {'x': x, 'adj': adj, 'L0_gnn_Wq': _L0_gnn_in['Wq'], 'L0_gnn_Wk': _L0_gnn_in['Wk'], 'L0_gnn_Wv': _L0_gnn_in['Wv'], 'L1_gnn_w3_w': _L1_gnn_in['w3_w'], 'L1_gnn_w3_b': _L1_gnn_in['w3_b'], 'L1_gnn_u3_w': _L1_gnn_in['u3_w'], 'L1_gnn_u3_b': _L1_gnn_in['u3_b'], 'L1_gnn_w4_w': _L1_gnn_in['w4_w'], 'L1_gnn_w4_b': _L1_gnn_in['w4_b'], 'L1_gnn_w5_w': _L1_gnn_in['w5_w'], 'L1_gnn_w5_b': _L1_gnn_in['w5_b'], 'L1_gnn_u5_w': _L1_gnn_in['u5_w'], 'L1_gnn_u5_b': _L1_gnn_in['u5_b']}

def reference(x, adj, L0_gnn_Wq, L0_gnn_Wk, L0_gnn_Wv, L1_gnn_w3_w, L1_gnn_w3_b, L1_gnn_u3_w, L1_gnn_u3_b, L1_gnn_w4_w, L1_gnn_w4_b, L1_gnn_w5_w, L1_gnn_w5_b, L1_gnn_u5_w, L1_gnn_u5_b):
    import jax
    import jax.numpy as jnp

    def _L0_gnn_ref(neuron_states, adjacency, Wq, Wk, Wv):
        import jax, jax.numpy as jnp
        import numpy as np
        B, N, D = (8, 1024, 256)
        q = jnp.einsum('bnd,ed->bne', neuron_states, Wq)
        k = jnp.einsum('bnd,ed->bne', neuron_states, Wk)
        v = jnp.einsum('bnd,ed->bne', neuron_states, Wv)
        rel = jnp.einsum('bnd,bmd->bnm', q, k)
        rel = adjacency.T[None, :, :] * rel
        rel = rel / jnp.linalg.norm(rel, axis=2, keepdims=True)
        return jnp.einsum('bnm,bmd->bnd', rel, v)

    def _L1_gnn_ref(x, in_mat, out_mat, w3_w, w3_b, u3_w, u3_b, w4_w, w4_b, w5_w, w5_b, u5_w, u5_b):
        import jax, jax.numpy as jnp
        import numpy as np
        B, N, D, T = (64, 128, 256, 3)

        def _lin(v, W, b):
            return jnp.einsum('...i,oi->...o', v, W) + b
        h = x
        for _ in range(T):
            a_in = jnp.einsum('nm,bmd->bnd', in_mat, h)
            a_out = jnp.einsum('nm,bmd->bnd', out_mat, h)
            av = jnp.concatenate([a_in, a_out], axis=-1)
            z = jax.nn.sigmoid(_lin(av, w3_w, w3_b) + _lin(h, u3_w, u3_b))
            r = jax.nn.sigmoid(_lin(av, w4_w, w4_b) + _lin(h, u3_w, u3_b))
            hv = jnp.tanh(_lin(av, w5_w, w5_b) + _lin(r * h, u5_w, u5_b))
            h = (1.0 - z) * h + z * hv
        return h
    h = jnp.maximum(_layernorm(x, axis=-1), 0.0)
    x = x + _L0_gnn_ref(h, adj, L0_gnn_Wq, L0_gnn_Wk, L0_gnn_Wv)
    h = jnp.maximum(_layernorm(x, axis=-1), 0.0)
    x = x + _L1_gnn_ref(h, adj, adj, L1_gnn_w3_w, L1_gnn_w3_b, L1_gnn_u3_w, L1_gnn_u3_b, L1_gnn_w4_w, L1_gnn_w4_b, L1_gnn_w5_w, L1_gnn_w5_b, L1_gnn_u5_w, L1_gnn_u5_b)
    return x

_drawn_inputs = setup_inputs


def setup_inputs(seed=0):
    import zlib

    import numpy as np

    out = dict(_drawn_inputs(seed))
    spreads = {'L1_gnn_w3_b': (0.0, 0.287),
     'L1_gnn_u3_b': (0.0, 0.282),
     'L1_gnn_w4_b': (0.0, 0.8),
     'L1_gnn_w5_b': (0.0, 0.1),
     'L1_gnn_u5_b': (0.0, 0.1)}
    factors = {}
    for name, (base, spread) in spreads.items():
        noise = np.random.default_rng([zlib.crc32(name.encode()), seed]).standard_normal(out[name].shape)
        drawn = base * np.exp(spread * noise) if base else spread * noise
        out[name] = jnp.asarray(drawn.astype(out[name].dtype))
    for name, factor in factors.items():
        out[name] = (out[name] * factor).astype(out[name].dtype)
    return out
```

```python
import concourse.bass as bass
from concourse import mybir
from contextlib import ExitStack



def gated_graph_kernel(nc, x, adj, adj_t, wq, wk, wv_t, w3_t, b3, u3_t, bu3, w4_t, b4, w5_t, b5,
                       u5_t, bu5, out):
    f32 = mybir.dt.float32
    f32r = mybir.dt.float32r
    ALU = mybir.AluOpType
    ACT = mybir.ActivationFunctionType

    P = 128
    B, N, D = x.shape
    C = D // P
    Q = 4
    T = Q * P
    G = B * N // T
    PAIRS = G // 2
    EPS = 1e-5

    x_g = x.rearrange("b n d -> (b n) d").rearrange("(g q p) d -> g p q d", q=Q, p=P)
    out_g = out.rearrange("b n d -> (b n) d").rearrange("(g q p) d -> g p q d", q=Q, p=P)

    TOK_START = ["split x 0", "v 0", "split x 1", "sum 0", "v 1", "new first", "sum 1", "new 0"]
    TOK_ROUND = ["step 1", "split x X", "step 2", "v X", "sum X", "step 3", "split x Y", "step 4",
                 "v Y", "sum Y", "final 5", "new 5", "final 0", "new 0"]
    TOK_END = ["step 1", "step 2", "step 3", "step 4", "final 5", "final 0"]
    FEA_START = ["q 0", "rel 0", "norm 0", "q 1", "rel 1", "adj first", "norm 1", "adj 0"]
    FEA_ROUND = ["adj 1", "q X", "adj 2", "rel X", "norm X", "adj 3", "q Y", "adj 4", "rel Y",
                 "norm Y", "adj 5", "adj 0"]
    FEA_END = ["adj 1", "adj 2", "adj 3", "adj 4"]

    def use_in_start(name):
        names = TOK_START if name in TOK_START else FEA_START
        return names.index(name)

    def use_in_round(name, i):
        names, first = (TOK_ROUND, len(TOK_START)) if name in TOK_ROUND else (FEA_ROUND, len(FEA_START))
        return i * len(names) + (first + names.index(name))

    def use_in_end(name):
        if name in TOK_END:
            return len(TOK_START) + (PAIRS - 1) * len(TOK_ROUND) + TOK_END.index(name)
        return len(FEA_START) + (PAIRS - 1) * len(FEA_ROUND) + FEA_END.index(name)

    ctx = ExitStack()
    with ctx:
        def sb(name, shape, dt=f32):
            return ctx.enter_context(nc.sbuf_tensor(name, shape, dt))

        def sem(name):
            return ctx.enter_context(nc.semaphore(name))

        names = ("m", "v", "u3", "w4", "wz", "w5", "u5")
        W_hi = {n: sb(f"W_hi_{n}", [P, C, D], f32r) for n in names}
        W_lo = {n: sb(f"W_lo_{n}", [P, C, D], f32r) for n in names}
        adjT = sb("adjT", [P, P])
        adjT_hi = sb("adjT_hi", [P, P], f32r)
        adjT_lo = sb("adjT_lo", [P, P], f32r)
        mask = sb("mask", [P, Q, P])
        ident = sb("ident", [P, P])
        ones = sb("ones", [P, 1])
        fence = sb("fence", [P, 3])
        minus_half = sb("minus_half", [P, Q])
        b_in = sb("b_in", [P, 5, C])
        b_r = sb("b_r", [P, C])
        b_z = sb("b_z", [P, C])
        b_c = sb("b_c", [P, C])

        x_s = [sb(f"x_s{s}", [P, Q, D]) for s in range(2)]
        resid = [sb(f"resid{s}", [P, Q, D]) for s in range(2)]
        h0 = [sb(f"h0{s}", [P, Q, D]) for s in range(2)]
        h = [sb(f"h{s}", [P, C, T]) for s in range(2)]
        h_hi = [sb(f"h_hi{s}", [P, C, T], f32r) for s in range(2)]
        h_lo = [sb(f"h_lo{s}", [P, C, T], f32r) for s in range(2)]
        a_hi = [sb(f"a_hi{s}", [P, C, T], f32r) for s in range(2)]
        a_lo = [sb(f"a_lo{s}", [P, C, T], f32r) for s in range(2)]
        o_s = [sb(f"o_s{s}", [P, Q, D]) for s in range(2)]

        t_hi = sb("t_hi", [P, Q, D], f32r)
        t_lo = sb("t_lo", [P, Q, D], f32r)
        r_s = sb("r_s", [P, C, T])
        z_s = sb("z_s", [P, C, T])
        c_s = sb("c_s", [P, C, T])
        d_s = sb("d_s", [P, C, T])
        rh = sb("rh", [P, C, T])
        rh_hi = sb("rh_hi", [P, C, T], f32r)
        rh_lo = sb("rh_lo", [P, C, T], f32r)

        hx = sb("hx", [P, Q, D])
        hxT_hi = sb("hxT_hi", [P, C, T], f32r)
        hxT_lo = sb("hxT_lo", [P, C, T], f32r)
        q_hi = sb("q_hi", [P, C, T], f32r)
        q_lo = sb("q_lo", [P, C, T], f32r)
        v_hi = sb("v_hi", [P, Q, D], f32r)
        v_lo = sb("v_lo", [P, Q, D], f32r)
        S = sb("S", [P, Q, P])
        S_hi = sb("S_hi", [P, Q, P], f32r)
        S_lo = sb("S_lo", [P, Q, P], f32r)
        S_sq = sb("S_sq", [P, Q, P])
        bn = [sb(f"bn{n}", [P, Q, 6]) for n in range(2)]
        mv = [sb(f"mv{n}", [P, Q, 2]) for n in range(2)]
        vare = [sb(f"vare{n}", [P, Q]) for n in range(2)]
        rstd = [sb(f"rstd{n}", [P, Q]) for n in range(2)]
        shift = [sb(f"shift{n}", [P, Q]) for n in range(2)]
        norm2 = sb("norm2", [P, Q])
        rnorm = sb("rnorm", [P, Q])

        raw = {"w3": r_s, "w4": z_s, "w5": c_s}
        raw["u3"], raw["u5"] = rh[:, 0, :], rh[:, 1, :]
        raw["q"], raw["k"] = d_s[:, 0, :], d_s[:, 1, :]
        raw["v"] = o_s[0][:, 0:2, :].rearrange("p a b -> p (a b)")
        sum4 = o_s[0][:, 2:4, :].rearrange("p a b -> p (a b)")
        sumz = o_s[1][:, 0:2, :].rearrange("p a b -> p (a b)")
        sum5 = o_s[1][:, 2:4, :].rearrange("p a b -> p (a b)")

        gate = ctx.enter_context(nc.psum_tensor("gate", [P, C, T], f32))
        cand = ctx.enter_context(nc.psum_tensor("cand", [P, C, T], f32))
        tok = ctx.enter_context(nc.psum_tensor("tok", [P, Q, D], f32))
        fea = ctx.enter_context(nc.psum_tensor("fea", [P, C, T], f32))
        tokT = tok[:].rearrange("p (c a) d -> p c (a d)", c=C)
        HQ = Q // 2

        attn_w_in, adj_in, gate_w_in, bias_in = sem("attn_w_in"), sem("adj_in"), sem("gate_w_in"), sem("bias_in")
        x_in = [sem("x_in0"), sem("x_in1")]
        stored = [sem("stored0"), sem("stored1")]
        const_zero, const_ready = sem("const_zero"), sem("const_ready")
        sum3_ready = sem("sum3_ready")
        m_full, w_sum, w_hi_ready, w_lo_ready, bias_ready = (
            sem("m_full"), sem("w_sum"), sem("w_hi_ready"), sem("w_lo_ready"), sem("bias_ready"))
        tok_full, tok_taken, fea_full, fea_taken = sem("tok_full"), sem("tok_taken"), sem("fea_full"), sem("fea_taken")
        r_full, z_full, c_full = sem("r_full"), sem("z_full"), sem("c_full")
        r_ready, z_ready, c_ready = sem("r_ready"), sem("z_ready"), sem("c_ready")
        rh_ready, rh_hi_ready, rh_lo_ready = sem("rh_ready"), sem("rh_hi_ready"), sem("rh_lo_ready")
        diff_ready, prod_ready, upd_ready = sem("diff_ready"), sem("prod_ready"), sem("upd_ready")
        h_hi_ready, t_hi_ready, a_hi_ready = sem("h_hi_ready"), sem("t_hi_ready"), sem("a_hi_ready")
        h_lo_ready = sem("h_lo_ready")
        h_new_ready = sem("h_new_ready")
        t_lo_ready = sem("t_lo_ready")
        resid_ready = sem("resid_ready")
        bn_ready = [sem("bn_ready0"), sem("bn_ready1")]
        mv_ready = [sem("mv_ready0"), sem("mv_ready1")]
        vare_ready = [sem("vare_ready0"), sem("vare_ready1")]
        rstd_ready = [sem("rstd_ready0"), sem("rstd_ready1")]
        shift_ready = [sem("shift_ready0"), sem("shift_ready1")]
        hx_ready, h0_ready = sem("hx_ready"), sem("h0_ready")
        hxT_hi_ready, q_hi_ready, v_hi_ready = sem("hxT_hi_ready"), sem("q_hi_ready"), sem("v_hi_ready")
        S_hi_ready, S_lo_ready, S_sq_ready = sem("S_hi_ready"), sem("S_lo_ready"), sem("S_sq_ready")
        rnorm_ready = sem("rnorm_ready")
        fence_done = [sem(f"fence_done{n}") for n in range(3)]

        block = ctx.enter_context(nc.Block())

        def graph_pair(q):
            return slice(q * P, (q + 1) * P)

        @block.sync
        def _(sp):
            def load_x(g, s):
                sp.dma_start(x_s[s][:], x_g[g]).then_inc(x_in[s], 16)

            def store(g, s, n_final):
                sp.wait_ge(tok_taken, 2 * n_final + 2)
                sp.dma_start(out_g[g], o_s[s][:]).then_inc(stored[s], 16)

            for s in range(2):
                sp.sem_inc(stored[s], 16)
            load_x(0, 0)
            sp.dma_start(raw["q"].rearrange("p (c n) -> p c n", c=C),
                         wq.rearrange("(c p) n -> p c n", p=P)).then_inc(attn_w_in, 16)
            sp.dma_start(raw["k"].rearrange("p (c n) -> p c n", c=C),
                         wk.rearrange("(c p) n -> p c n", p=P)).then_inc(attn_w_in, 16)
            sp.dma_start(raw["v"].rearrange("p (c n) -> p c n", c=C),
                         wv_t.rearrange("(c p) n -> p c n", p=P)).then_inc(attn_w_in, 16)
            load_x(1, 1)
            sp.wait_ge(const_zero, 1)
            for e in range(2):
                part = slice(e * N, (e + 1) * N)
                sp.dma_start(adjT[part, part], adj_t).then_inc(adj_in, 16)
                for q in range(Q):
                    sp.dma_start(mask[part, q, part], adj).then_inc(adj_in, 16)
            for name, src in (("w4", w4_t), ("w3", w3_t), ("w5", w5_t)):
                sp.dma_start(raw[name][:].rearrange("p a (c n) -> p (a c) n", n=D),
                             src.rearrange("(c p) n -> p c n", p=P)).then_inc(gate_w_in, 16)
            for name, src in (("u3", u3_t), ("u5", u5_t)):
                sp.dma_start(raw[name].rearrange("p (c n) -> p c n", c=C),
                             src.rearrange("(c p) n -> p c n", p=P)).then_inc(gate_w_in, 16)
            for n, src in enumerate((b3, bu3, b4, b5, bu5)):
                sp.dma_start(b_in[:, n, :], src).then_inc(bias_in, 16)

            with sp.Fori(0, PAIRS - 1) as i:
                for s in range(2):
                    sp.wait_ge(resid_ready, 2 * i + (s + 1))
                    load_x(2 * i + 2 + s, s)
                store(2 * i, 0, use_in_round("final 5", i))
                store(2 * i + 1, 1, use_in_round("final 0", i))
            store(G - 2, 0, use_in_end("final 5"))
            store(G - 1, 1, use_in_end("final 0"))
            for s in range(2):
                sp.wait_ge(stored[s], 16 * PAIRS + 16)

        @block.gpsimd
        def _(pool):
            nc.gpsimd.memset(adjT[:], 0.0)
            nc.gpsimd.memset(mask[:], 0.0).then_inc(const_zero, 1)
            nc.gpsimd.memset(ones[:], 1.0)
            nc.gpsimd.memset(minus_half[:], -0.5)
            nc.gpsimd.memset(ident[:], 0.0).then_inc(const_zero, 1)
            pool.wait_ge(const_zero, 2)
            nc.gpsimd.affine_select(out=ident[:], in_=ident[:], compare_op=ALU.not_equal, fill=1.0,
                                    base=0, pattern=[[-1, P]], channel_multiplier=1).then_inc(const_ready, 1)

            def inverse_std(n, g):
                pool.wait_ge(vare_ready[n], g + 1)
                nc.gpsimd.tensor_tensor(rstd[n][:], vare[n][:], minus_half[:], ALU.pow).then_inc(rstd_ready[n], 1)

            def inverse_norm(n):
                pool.wait_ge(fea_taken, 2 * n + 2)
                nc.gpsimd.tensor_tensor(rnorm[:], norm2[:], minus_half[:], ALU.pow).then_inc(rnorm_ready, 1)

            def keep_resid(g, s, n_final):
                pool.wait_ge(h0_ready, Q * (g + 1))
                if n_final is not None:
                    pool.wait_ge(tok_taken, 2 * n_final + 2)
                pool.wait_ge(fence_done[2], g)
                nc.gpsimd.tensor_tensor(fence[:, 2:3], ones[:], ones[:], ALU.mult).then_inc(fence_done[2], 1)
                nc.gpsimd.tensor_copy(resid[s][:], x_s[s][:]).then_inc(resid_ready, 1)

            n = use_in_start
            inverse_std(0, 0)
            inverse_std(0, 1)
            inverse_norm(n("norm 0"))
            inverse_std(1, 0)
            keep_resid(0, 0, None)
            inverse_norm(n("norm 1"))
            inverse_std(1, 1)
            keep_resid(1, 1, None)
            with pool.Fori(0, PAIRS - 1) as i:
                inverse_std(0, 2 * i + 2)
                inverse_std(0, 2 * i + 3)
                inverse_norm(use_in_round("norm X", i))
                inverse_std(1, 2 * i + 2)
                inverse_norm(use_in_round("norm Y", i))
                inverse_std(1, 2 * i + 3)
                keep_resid(2 * i + 2, 0, use_in_round("final 5", i))
                keep_resid(2 * i + 3, 1, use_in_round("final 0", i))

        @block.tensor
        def _(pe):
            def product(dst, lhs, rhs, start, stop):
                (l_hi, l_lo), (r_hi, r_lo) = lhs, rhs
                nc.tensor.matmul(dst, l_hi, r_hi, start=start, stop=False, skip_group_check=True)
                nc.tensor.matmul(dst, l_hi, r_lo, start=False, stop=False, skip_group_check=True)
                return nc.tensor.matmul(dst, l_lo, r_hi, start=False, stop=stop, skip_group_check=True)

            def weight(n, c, o):
                return W_hi[n][:, c, o * P:(o + 1) * P], W_lo[n][:, c, o * P:(o + 1) * P]

            def linear(dst, n, o, hi, lo, start, stop):
                for c in range(C):
                    last = product(dst, weight(n, c, o), (hi[:, c, :], lo[:, c, :]),
                                   start and c == 0, stop and c == C - 1)
                return last

            def tok_wait(n, b):
                if isinstance(n, int) and n == 0:
                    return
                pe.wait_ge(tok_taken, 2 * n + (b - 1))

            def fea_wait(n, b):
                if isinstance(n, int) and n == 0:
                    return
                pe.wait_ge(fea_taken, 2 * n + (b - 1))

            def transpose_hx(g, n):
                pe.wait_ge(hx_ready, Q * (g + 1))
                for c in range(C):
                    tok_wait(n, c)
                    for q in range(Q):
                        last = nc.tensor.transpose(tokT[:, c, graph_pair(q)], hx[:, q, c * P:(c + 1) * P], ident[:])
                    last.then_inc(tok_full, 1)

            def queries(g, n, n_hx):
                pe.wait_ge(hxT_hi_ready, 2 * g + 2)
                pe.wait_ge(tok_taken, 2 * n_hx + 2)
                for c in range(C):
                    fea_wait(n, c)
                    linear(fea[:, c, :], "m", c, hxT_hi, hxT_lo, True, True).then_inc(fea_full, 1)

            def values(g, n):
                for b in range(2):
                    tok_wait(n, b)
                    for q in range(HQ * b, HQ * b + HQ):
                        for c in range(C):
                            last = product(tok[:, q, :], (hxT_hi[:, c, graph_pair(q)], hxT_lo[:, c, graph_pair(q)]),
                                           (W_hi["v"][:, c, :], W_lo["v"][:, c, :]), c == 0, c == C - 1)
                    last.then_inc(tok_full, 1)

            def scores(g, n, n_q):
                pe.wait_ge(q_hi_ready, 2 * g + 2)
                pe.wait_ge(fea_taken, 2 * n_q + 2)
                fea_wait(n, 0)
                for q in range(Q):
                    for c in range(C):
                        last = product(fea[:, 0, graph_pair(q)], (hxT_hi[:, c, graph_pair(q)], hxT_lo[:, c, graph_pair(q)]),
                                       (q_hi[:, c, graph_pair(q)], q_lo[:, c, graph_pair(q)]), c == 0, c == C - 1)
                last.then_inc(fea_full, 2)

            def weighted_sum(g, n_tok, n_fea, n_v):
                pe.wait_ge(S_sq_ready, g + 1)
                fea_wait(n_fea, 1)
                for q in range(Q):
                    last = nc.tensor.matmul(fea[:, 1, q:q + 1], S_sq[:, q, :], ones[:], start=True, stop=True)
                last.then_inc(fea_full, 2)
                pe.wait_ge(S_hi_ready, g + 1)
                pe.wait_ge(S_lo_ready, g + 1)
                pe.wait_ge(v_hi_ready, 2 * g + 2)
                pe.wait_ge(tok_taken, 2 * n_v + 2)
                for b in range(2):
                    tok_wait(n_tok, b)
                    for q in range(HQ * b, HQ * b + HQ):
                        last = product(tok[:, q, :], (S_hi[:, q, :], S_lo[:, q, :]),
                                       (v_hi[:, q, :], v_lo[:, q, :]), True, True)
                    last.then_inc(tok_full, 1)

            def transpose_state(w, o, n):
                pe.wait_ge(upd_ready, 2 * w)
                for b in range(2):
                    tok_wait(n, b)
                    for q in range(HQ * b, HQ * b + HQ):
                        for c in range(C):
                            last = nc.tensor.transpose(tok[:, q, c * P:(c + 1) * P], h[o][:, c, graph_pair(q)], ident[:])
                    last.then_inc(tok_full, 1)

            def adjacency(v, n):
                pe.wait_ge(t_hi_ready, 2 * v + 2)
                for c in range(C):
                    fea_wait(n, c)
                    for q in range(Q):
                        last = product(fea[:, c, graph_pair(q)], (t_hi[:, q, c * P:(c + 1) * P], t_lo[:, q, c * P:(c + 1) * P]),
                                       (adjT_hi[:], adjT_lo[:]), True, True)
                    last.then_inc(fea_full, 1)

            def transpose_new(g, s, n):
                for c in range(C):
                    tok_wait(n, c)
                    for q in range(Q):
                        last = nc.tensor.transpose(tokT[:, c, graph_pair(q)], h0[s][:, q, c * P:(c + 1) * P], ident[:])
                    last.then_inc(tok_full, 1)

            def reset_gate(w, s, n_adj):
                pe.wait_ge(h_hi_ready, 2 * w + 2)
                for o in range(C):
                    if not (isinstance(w, int) and w == 0):
                        pe.wait_ge(z_ready, 2 * w + (o - 1))
                    linear(gate[:, o, :], "u3", o, h_hi[s], h_lo[s], True, False)
                    if o == 0:
                        pe.wait_ge(a_hi_ready, 2 * w + 2)
                        pe.wait_ge(fea_taken, 2 * n_adj + 2)
                    linear(gate[:, o, :], "w4", o, a_hi[s], a_lo[s], False, True).then_inc(r_full, 1)

            def update_gate(w, s):
                for o in range(C):
                    pe.wait_ge(r_ready, 2 * w + (o + 1))
                    linear(gate[:, o, :], "wz", o, a_hi[s], a_lo[s], False, True).then_inc(z_full, 1)

            def candidate_a(w, s):
                for o in range(C):
                    if not (isinstance(w, int) and w == 0):
                        pe.wait_ge(c_ready, 2 * w + (o - 1))
                    linear(cand[:, o, :], "w5", o, a_hi[s], a_lo[s], True, False)

            def candidate_rh(w, s):
                pe.wait_ge(rh_hi_ready, 2 * w + 2)
                pe.wait_ge(rh_lo_ready, 2 * w + 2)
                for o in range(C):
                    linear(cand[:, o, :], "u5", o, rh_hi, rh_lo, False, True).then_inc(c_full, 1)

            def window(i, k, use, attention=True, final=True, new=True):
                w, s, o = 6 * i + k, k % 2, 1 - k % 2
                first = isinstance(i, int) and i == 0 and k == 0
                if first:
                    n_adj, n_new = use("adj first"), use("new first")
                elif k == 1:
                    n_adj, n_new = use_in_round("adj 0", i - 1), use_in_round("new 0", i - 1)
                else:
                    n_adj, n_new = use(f"adj {(k - 1) % 6}"), use("new 5") if k == 0 else None
                if attention and k == 2:
                    queries(2 * i + 2, use("q X"), use("split x X"))
                if attention and k == 4:
                    queries(2 * i + 3, use("q Y"), use("split x Y"))
                if attention and k == 3:
                    weighted_sum(2 * i + 2, use("sum X"), use("norm X"), use("v X"))
                if attention and k == 5:
                    weighted_sum(2 * i + 3, use("sum Y"), use("norm Y"), use("v Y"))
                if k in (0, 1):
                    pe.wait_ge(tok_taken, 2 * n_new + 2)
                else:
                    pe.wait_ge(h_lo_ready, 8 * i + (2 * k - 2))
                reset_gate(w, s, n_adj)
                if k in (5, 0):
                    if final:
                        transpose_state(w, o, use(f"final {k}"))
                else:
                    transpose_state(w, o, use(f"step {k}"))
                update_gate(w, s)
                if new:
                    if k in (5, 0):
                        g_new = 2 * i + 2 if k == 5 else 2 * i + 1
                        pe.wait_ge(t_lo_ready, 2 * g_new + 2)
                        adjacency(w + 1, use(f"adj {k}"))
                        transpose_new(g_new, o, use(f"new {k}"))
                    else:
                        pe.wait_ge(tok_taken, 2 * use(f"step {k}") + 2)
                        adjacency(w + 1, use(f"adj {k}"))
                candidate_a(w, s)
                if attention and k == 1:
                    transpose_hx(2 * i + 2, use("split x X"))
                if attention and k == 3:
                    transpose_hx(2 * i + 3, use("split x Y"))
                if attention and k == 2:
                    values(2 * i + 2, use("v X"))
                    scores(2 * i + 2, use("rel X"), use("q X"))
                if attention and k == 4:
                    values(2 * i + 3, use("v Y"))
                    scores(2 * i + 3, use("rel Y"), use("q Y"))
                candidate_rh(w, s)

            pe.wait_ge(attn_w_in, 48)
            for c in range(C):
                for e in range(C):
                    last = nc.tensor.matmul(gate[:, 0, c * D:(c + 1) * D], raw["q"][:, e * D + c * P:e * D + (c + 1) * P],
                                            raw["k"][:, e * D:(e + 1) * D], start=e == 0, stop=e == C - 1)
            last.then_inc(m_full, 1)
            pe.wait_ge(const_ready, 1)
            n = use_in_start
            transpose_hx(0, n("split x 0"))
            pe.wait_ge(w_lo_ready, 1)
            queries(0, n("q 0"), n("split x 0"))
            pe.wait_ge(w_lo_ready, 2)
            values(0, n("v 0"))
            scores(0, n("rel 0"), n("q 0"))
            transpose_hx(1, n("split x 1"))
            weighted_sum(0, n("sum 0"), n("norm 0"), n("v 0"))
            queries(1, n("q 1"), n("split x 1"))
            values(1, n("v 1"))
            scores(1, n("rel 1"), n("q 1"))
            pe.wait_ge(w_lo_ready, 3)
            pe.wait_ge(t_lo_ready, 2)
            adjacency(0, n("adj first"))
            transpose_new(0, 0, n("new first"))
            weighted_sum(1, n("sum 1"), n("norm 1"), n("v 1"))
            pe.wait_ge(w_lo_ready, len(names) + 1)
            window(0, 0, n, attention=False, final=False)
            with pe.Fori(0, PAIRS - 1) as i:
                for k in (1, 2, 3, 4, 5):
                    window(i, k, lambda name: use_in_round(name, i))
                window(i + 1, 0, lambda name: use_in_round(name, i), attention=False)
            for k in (1, 2, 3, 4):
                window(PAIRS - 1, k, use_in_end, attention=False)
            window(PAIRS - 1, 5, use_in_end, attention=False, new=False)
            transpose_state(6 * PAIRS, 1, use_in_end("final 0"))

        @block.scalar
        def _(act):
            def copy(dst, src):
                return nc.scalar.activation(dst, src, ACT.Copy)

            def tok_wait(n, b):
                act.wait_ge(tok_full, 2 * n + (b + 1))

            def fea_wait(n, b):
                act.wait_ge(fea_full, 2 * n + (b + 1))

            def split_weight(n, hi, src):
                act.wait_ge(w_sum, n)
                copy(hi, src).then_inc(w_hi_ready, 1)

            def normalise(n, g, s):
                act.wait_ge(shift_ready[n], g + 1)
                dst, done = (hx, hx_ready) if n == 0 else (h0[s], h0_ready)
                for q in range(Q):
                    nc.scalar.activation(dst[:, q, :], x_s[s][:, q, :], ACT.Relu, bias=shift[n][:, q:q + 1],
                                         scale=rstd[n][:, q:q + 1]).then_inc(done, 1)

            def split_hx(n):
                for c in range(C):
                    tok_wait(n, c)
                    copy(hxT_hi[:, c, :], tokT[:, c, :]).then_inc(hxT_hi_ready, 1)

            def split_q(n):
                for c in range(C):
                    fea_wait(n, c)
                    copy(q_hi[:, c, :], fea[:, c, :]).then_inc(q_hi_ready, 1)

            def split_v(n):
                for b in range(2):
                    tok_wait(n, b)
                    copy(v_hi[:, HQ * b:HQ * b + HQ, :], tok[:, HQ * b:HQ * b + HQ, :]).then_inc(v_hi_ready, 1)

            def split_S(n):
                act.wait_ge(fea_taken, 2 * n + 2)
                copy(S_hi[:], S[:]).then_inc(S_hi_ready, 1)
                nc.scalar.activation(S_sq[:], S[:], ACT.Square).then_inc(S_sq_ready, 1)

            def split_state(w, o):
                for c in range(C):
                    act.wait_ge(upd_ready, 2 * w + (c - 1))
                    copy(h_hi[o][:, c, :], h[o][:, c, :]).then_inc(h_hi_ready, 1)

            def split_tok(n):
                for b in range(2):
                    tok_wait(n, b)
                    copy(t_hi[:, HQ * b:HQ * b + HQ, :], tok[:, HQ * b:HQ * b + HQ, :]).then_inc(t_hi_ready, 1)

            def split_h0(g, s):
                for b in range(2):
                    act.wait_ge(h0_ready, Q * g + HQ * (b + 1))
                    copy(t_hi[:, HQ * b:HQ * b + HQ, :], h0[s][:, HQ * b:HQ * b + HQ, :]).then_inc(t_hi_ready, 1)

            def split_a(s, n):
                for c in range(C):
                    fea_wait(n, c)
                    copy(a_hi[s][:, c, :], fea[:, c, :]).then_inc(a_hi_ready, 1)

            def split_new(s, n):
                for c in range(C):
                    tok_wait(n, c)
                    copy(h_hi[s][:, c, :], tokT[:, c, :]).then_inc(h_hi_ready, 1)

            def window(i, k, use, attention=True, final=True, new=True):
                w, s, o = 6 * i + k, k % 2, 1 - k % 2
                g_att = {1: ("X", 2 * i + 2), 2: ("X", 2 * i + 2), 3: ("Y", 2 * i + 3), 4: ("Y", 2 * i + 3)}.get(k)
                if attention and k in (2, 4):
                    split_q(use(f"q {g_att[0]}"))
                if k in (5, 0):
                    g_new = 2 * i + 2 if k == 5 else 2 * i + 1
                    if new:
                        split_h0(g_new, o)
                else:
                    split_state(w, o)
                for c in range(C):
                    act.wait_ge(r_full, 2 * w + (c + 1))
                    nc.scalar.activation(r_s[:, c, :], gate[:, c, :], ACT.Sigmoid,
                                         bias=b_r[:, c:c + 1]).then_inc(r_ready, 1)
                if k not in (5, 0):
                    split_tok(use(f"step {k}"))
                for c in range(C):
                    act.wait_ge(rh_ready, 2 * w + (c + 1))
                    copy(rh_hi[:, c, :], rh[:, c, :]).then_inc(rh_hi_ready, 1)
                if not (isinstance(w, int) and w == 0):
                    act.wait_ge(upd_ready, 2 * w)
                for c in range(C):
                    act.wait_ge(z_full, 2 * w + (c + 1))
                    nc.scalar.activation(z_s[:, c, :], gate[:, c, :], ACT.Sigmoid,
                                         bias=b_z[:, c:c + 1]).then_inc(z_ready, 1)
                if new:
                    split_a(o, use(f"adj {k}"))
                    if k in (5, 0):
                        split_new(o, use(f"new {k}"))
                if attention and k == 1:
                    normalise(0, 2 * i + 2, 0)
                if attention and k == 2:
                    normalise(0, 2 * i + 3, 1)
                if attention and k == 3:
                    normalise(1, 2 * i + 2, 0)
                if attention and k == 5:
                    normalise(1, 2 * i + 3, 1)
                if attention and k in (1, 3):
                    split_hx(use(f"split x {g_att[0]}"))
                if attention and k in (2, 4):
                    split_v(use(f"v {g_att[0]}"))
                    split_S(use(f"rel {g_att[0]}"))
                for c in range(C):
                    act.wait_ge(c_full, 2 * w + (c + 1))
                    nc.scalar.activation(c_s[:, c, :], cand[:, c, :], ACT.Tanh,
                                         bias=b_c[:, c:c + 1]).then_inc(c_ready, 1)

            n = use_in_start
            normalise(0, 0, 0)
            act.wait_ge(m_full, 1)
            split_weight(0, W_hi["m"][:].rearrange("p c n -> p (c n)"), gate[:, 0, :])
            split_hx(n("split x 0"))
            act.wait_ge(attn_w_in, 48)
            split_weight(0, W_hi["v"][:].rearrange("p c n -> p (c n)"), raw["v"])
            split_q(n("q 0"))
            normalise(0, 1, 1)
            split_v(n("v 0"))
            split_S(n("rel 0"))
            split_hx(n("split x 1"))
            act.wait_ge(adj_in, 16 * 2 * (1 + Q))
            split_weight(0, adjT_hi[:], adjT[:])
            split_q(n("q 1"))
            normalise(1, 0, 0)
            split_v(n("v 1"))
            split_S(n("rel 1"))
            split_h0(0, 0)
            act.wait_ge(gate_w_in, 16 * 5)
            for m, (name, src) in enumerate((("u3", raw["u3"]), ("w4", sum4), ("wz", sumz), ("w5", sum5), ("u5", raw["u5"]))):
                split_weight({"w4": 1, "wz": 2, "w5": 3}.get(name, 0), W_hi[name][:].rearrange("p c n -> p (c n)"), src)
            split_a(0, n("adj first"))
            split_new(0, n("new first"))
            normalise(1, 1, 1)
            act.wait_ge(bias_ready, 3)
            window(0, 0, n, attention=False, final=False)
            with act.Fori(0, PAIRS - 1) as i:
                for k in (1, 2, 3, 4, 5):
                    window(i, k, lambda name: use_in_round(name, i))
                window(i + 1, 0, lambda name: use_in_round(name, i), attention=False)
            for k in (1, 2, 3, 4):
                window(PAIRS - 1, k, use_in_end, attention=False)
            window(PAIRS - 1, 5, use_in_end, attention=False, new=False)

        @block.vector
        def _(dve):
            def sub(dst, a, b):
                return nc.vector.tensor_tensor(dst, a, b, ALU.subtract)

            def tok_wait(n, b):
                dve.wait_ge(tok_full, 2 * n + (b + 1))

            def fea_wait(n, b):
                dve.wait_ge(fea_full, 2 * n + (b + 1))

            def split_weight(n, lo, src, hi):
                dve.wait_ge(w_hi_ready, n)
                sub(lo, src, hi).then_inc(w_lo_ready, 1)

            def statistics(n, g, s, at):
                if n == 0:
                    dve.wait_ge(x_in[s], 16 * at)
                else:
                    dve.wait_ge(tok_taken, 2 * at + 2)
                for q in range(Q):
                    nc.vector.bn_stats(bn[n][:, q, :], x_s[s][:, q, :]).then_inc(bn_ready[n], 1)
                dve.wait_ge(bn_ready[n], Q * (g + 1))
                dve.wait_ge(fence_done[n], g)
                nc.vector.memset(fence[:, n:n + 1], 0.0).then_inc(fence_done[n], 1)
                for q in range(Q):
                    nc.vector.bn_aggr(mv[n][:, q, :], bn[n][:, q, :]).then_inc(mv_ready[n], 1)
                dve.wait_ge(mv_ready[n], Q * (g + 1))
                nc.vector.tensor_scalar(vare[n][:], mv[n][:, :, 1], EPS, None, ALU.add).then_inc(vare_ready[n], 1)

            def shifts(n, g):
                dve.wait_ge(rstd_ready[n], g + 1)
                nc.vector.scalar_tensor_tensor(shift[n][:], mv[n][:, :, 0], -1.0, rstd[n][:],
                                               ALU.mult, ALU.mult).then_inc(shift_ready[n], 1)

            def split_hx(g, n):
                for c in range(C):
                    tok_wait(n, c)
                    dve.wait_ge(hxT_hi_ready, 2 * g + (c + 1))
                    sub(hxT_lo[:, c, :], tokT[:, c, :], hxT_hi[:, c, :]).then_inc(tok_taken, 1)

            def split_q(g, n):
                for c in range(C):
                    fea_wait(n, c)
                    dve.wait_ge(q_hi_ready, 2 * g + (c + 1))
                    sub(q_lo[:, c, :], fea[:, c, :], q_hi[:, c, :]).then_inc(fea_taken, 1)

            def split_v(g, n):
                for b in range(2):
                    part = slice(HQ * b, HQ * b + HQ)
                    tok_wait(n, b)
                    dve.wait_ge(v_hi_ready, 2 * g + (b + 1))
                    sub(v_lo[:, part, :], tok[:, part, :], v_hi[:, part, :]).then_inc(tok_taken, 1)

            def mask_scores(n):
                fea_wait(n, 1)
                nc.vector.tensor_tensor(S[:].rearrange("p q n -> p (q n)"), fea[:, 0, :],
                                        mask[:].rearrange("p q n -> p (q n)"), ALU.mult).then_inc(fea_taken, 2)

            def split_S(g, n):
                dve.wait_ge(fea_taken, 2 * n + 2)
                dve.wait_ge(S_hi_ready, g + 1)
                sub(S_lo[:], S[:], S_hi[:]).then_inc(S_lo_ready, 1)

            def take_norm(n):
                fea_wait(n, 1)
                nc.vector.tensor_copy(norm2[:], fea[:, 1, 0:Q]).then_inc(fea_taken, 2)

            def add_attention(g, s, n):
                dve.wait_ge(rnorm_ready, g + 1)
                for q in range(Q):
                    tok_wait(n, q // HQ)
                    last = nc.vector.scalar_tensor_tensor(x_s[s][:, q, :], tok[:, q, :], rnorm[:, q:q + 1],
                                                          x_s[s][:, q, :], ALU.mult, ALU.add)
                    if q % HQ == HQ - 1:
                        last.then_inc(tok_taken, 1)

            def split_state(w, o):
                for c in range(C):
                    dve.wait_ge(h_hi_ready, 2 * w + (c + 3))
                    sub(h_lo[o][:, c, :], h[o][:, c, :], h_hi[o][:, c, :]).then_inc(h_lo_ready, 1)

            def split_tok(v, n):
                for b in range(2):
                    part = slice(HQ * b, HQ * b + HQ)
                    tok_wait(n, b)
                    dve.wait_ge(t_hi_ready, 2 * v + (b + 1))
                    sub(t_lo[:, part, :], tok[:, part, :], t_hi[:, part, :]).then_inc(tok_taken, 1)

            def split_h0(v, s):
                for b in range(2):
                    part = slice(HQ * b, HQ * b + HQ)
                    dve.wait_ge(t_hi_ready, 2 * v + (b + 1))
                    sub(t_lo[:, part, :], h0[s][:, part, :], t_hi[:, part, :]).then_inc(t_lo_ready, 1)

            def split_a(v, s, n):
                for c in range(C):
                    fea_wait(n, c)
                    dve.wait_ge(a_hi_ready, 2 * v + (c + 1))
                    sub(a_lo[s][:, c, :], fea[:, c, :], a_hi[s][:, c, :]).then_inc(fea_taken, 1)

            def take_new(v, g, s, n):
                for c in range(C):
                    dve.wait_ge(h_hi_ready, 2 * v + (c + 1))
                    nc.vector.tensor_copy(h[s][:, c, :], tokT[:, c, :]).then_inc(h_new_ready, 1)
                    sub(h_lo[s][:, c, :], tokT[:, c, :], h_hi[s][:, c, :]).then_inc(tok_taken, 1)

            def add_resid(g, s, n, stores):
                dve.wait_ge(resid_ready, g + 1)
                dve.wait_ge(stored[s], stores * 16 + 16)
                for b in range(2):
                    part = slice(HQ * b, HQ * b + HQ)
                    tok_wait(n, b)
                    nc.vector.tensor_tensor(o_s[s][:, part, :], tok[:, part, :], resid[s][:, part, :],
                                            ALU.add).then_inc(tok_taken, 1)

            def update(w, o):
                for c in range(C):
                    dve.wait_ge(c_ready, 2 * w + (c - 1))
                    sub(d_s[:, c, :], c_s[:, c, :], h[o][:, c, :]).then_inc(diff_ready, 1)
                for c in range(C):
                    dve.wait_ge(z_ready, 2 * w + (c - 1))
                    dve.wait_ge(diff_ready, 2 * w + (c - 1))
                    nc.vector.tensor_tensor(d_s[:, c, :], z_s[:, c, :], d_s[:, c, :], ALU.mult).then_inc(prod_ready, 1)
                for c in range(C):
                    dve.wait_ge(prod_ready, 2 * w + (c - 1))
                    nc.vector.tensor_tensor(h[o][:, c, :], h[o][:, c, :], d_s[:, c, :], ALU.add).then_inc(upd_ready, 1)

            def window(i, k, use, attention=True, final=True, new=True):
                w, s, o = 6 * i + k, k % 2, 1 - k % 2
                g_att = {1: ("X", 2 * i + 2), 2: ("X", 2 * i + 2), 3: ("Y", 2 * i + 3), 4: ("Y", 2 * i + 3)}.get(k)
                if not (isinstance(w, int) and w == 0):
                    update(w, o)
                if attention and k in (2, 4):
                    split_q(g_att[1], use(f"q {g_att[0]}"))
                if attention and k == 3:
                    take_norm(use("norm X"))
                if attention and k == 5:
                    take_norm(use("norm Y"))
                if k in (5, 0):
                    if new:
                        split_h0(w + 1, o)
                else:
                    split_state(w, o)
                if attention and k == 3:
                    add_attention(2 * i + 2, 0, use("sum X"))
                if attention and k == 5:
                    add_attention(2 * i + 3, 1, use("sum Y"))
                for c in range(C):
                    dve.wait_ge(r_ready, 2 * w + (c + 1))
                    if s == 0:
                        dve.wait_ge(h_new_ready, 4 * i + (c + 1))
                    elif k == 1:
                        dve.wait_ge(h_new_ready, 4 * i + (c + 3))
                    nc.vector.tensor_tensor(rh[:, c, :], r_s[:, c, :], h[s][:, c, :], ALU.mult).then_inc(rh_ready, 1)
                if k in (5, 0):
                    if final:
                        add_resid(2 * i if k == 5 else 2 * i - 1, o, use(f"final {k}"), i if k == 5 else i - 1)
                else:
                    split_tok(w + 1, use(f"step {k}"))
                for c in range(C):
                    dve.wait_ge(rh_hi_ready, 2 * w + (c + 1))
                    sub(rh_lo[:, c, :], rh[:, c, :], rh_hi[:, c, :]).then_inc(rh_lo_ready, 1)
                if attention and k == 1:
                    statistics(0, 2 * i + 2, 0, i + 2)
                if attention and k == 3:
                    statistics(1, 2 * i + 2, 0, use("sum X"))
                if attention and k == 5:
                    statistics(1, 2 * i + 3, 1, use("sum Y"))
                if new:
                    split_a(w + 1, o, use(f"adj {k}"))
                if attention and k == 1:
                    shifts(0, 2 * i + 2)
                if attention and k == 2:
                    statistics(0, 2 * i + 3, 1, i + 2)
                    shifts(0, 2 * i + 3)
                if attention and k == 3:
                    shifts(1, 2 * i + 2)
                if attention and k == 5:
                    shifts(1, 2 * i + 3)
                if new:
                    if k in (5, 0):
                        take_new(w + 1, 2 * i + 2 if k == 5 else 2 * i + 1, o, use(f"new {k}"))
                if attention and k in (1, 3):
                    split_hx(g_att[1], use(f"split x {g_att[0]}"))
                if attention and k in (2, 4):
                    split_v(g_att[1], use(f"v {g_att[0]}"))
                    mask_scores(use(f"rel {g_att[0]}"))
                    split_S(g_att[1], use(f"rel {g_att[0]}"))

            n = use_in_start
            flat = "p c n -> p (c n)"
            statistics(0, 0, 0, 1)
            shifts(0, 0)
            dve.wait_ge(m_full, 1)
            split_weight(1, W_lo["m"][:].rearrange(flat), gate[:, 0, :], W_hi["m"][:].rearrange(flat))
            split_hx(0, n("split x 0"))
            split_weight(2, W_lo["v"][:].rearrange(flat), raw["v"], W_hi["v"][:].rearrange(flat))
            statistics(0, 1, 1, 1)
            shifts(0, 1)
            split_q(0, n("q 0"))
            split_v(0, n("v 0"))
            dve.wait_ge(adj_in, 16 * 2 * (1 + Q))
            mask_scores(n("rel 0"))
            split_S(0, n("rel 0"))
            split_hx(1, n("split x 1"))
            split_weight(3, adjT_lo[:], adjT[:], adjT_hi[:])
            take_norm(n("norm 0"))
            add_attention(0, 0, n("sum 0"))
            statistics(1, 0, 0, n("sum 0"))
            shifts(1, 0)
            split_q(1, n("q 1"))
            split_v(1, n("v 1"))
            mask_scores(n("rel 1"))
            split_S(1, n("rel 1"))
            split_h0(0, 0)
            dve.wait_ge(gate_w_in, 16 * 5)
            nc.vector.tensor_tensor(sum4, raw["w4"][:, 0, :], raw["w4"][:, 1, :], ALU.add).then_inc(w_sum, 1)
            dve.wait_ge(w_sum, 1)
            nc.vector.tensor_tensor(sumz, raw["w3"][:, 0, :], raw["w3"][:, 1, :], ALU.add).then_inc(sum3_ready, 1)
            dve.wait_ge(sum3_ready, 1)
            sub(sumz, sumz, sum4).then_inc(w_sum, 1)
            nc.vector.tensor_tensor(sum5, raw["w5"][:, 0, :], raw["w5"][:, 1, :], ALU.add).then_inc(w_sum, 1)
            dve.wait_ge(w_sum, 3)
            for m, (name, src) in enumerate((("u3", raw["u3"]), ("w4", sum4), ("wz", sumz), ("w5", sum5), ("u5", raw["u5"]))):
                split_weight(4 + m, W_lo[name][:].rearrange(flat), src, W_hi[name][:].rearrange(flat))
            dve.wait_ge(bias_in, 16 * 5)
            for dst, (m1, m2) in ((b_r, (2, 1)), (b_z, (0, 1)), (b_c, (3, 4))):
                nc.vector.tensor_tensor(dst[:], b_in[:, m1, :], b_in[:, m2, :], ALU.add).then_inc(bias_ready, 1)
            split_a(0, 0, n("adj first"))
            take_new(0, 0, 0, n("new first"))
            take_norm(n("norm 1"))
            add_attention(1, 1, n("sum 1"))
            statistics(1, 1, 1, n("sum 1"))
            shifts(1, 1)
            window(0, 0, n, attention=False, final=False)
            with dve.Fori(0, PAIRS - 1) as i:
                for k in (1, 2, 3, 4, 5):
                    window(i, k, lambda name: use_in_round(name, i))
                window(i + 1, 0, lambda name: use_in_round(name, i), attention=False)
            for k in (1, 2, 3, 4):
                window(PAIRS - 1, k, use_in_end, attention=False)
            window(PAIRS - 1, 5, use_in_end, attention=False, new=False)
            update(6 * PAIRS, 1)
            add_resid(G - 1, 1, use_in_end("final 0"), PAIRS - 1)


def kernel(x, adj, L0_gnn_Wq, L0_gnn_Wk, L0_gnn_Wv, L1_gnn_w3_w, L1_gnn_w3_b, L1_gnn_u3_w, L1_gnn_u3_b,
           L1_gnn_w4_w, L1_gnn_w4_b, L1_gnn_w5_w, L1_gnn_w5_b, L1_gnn_u5_w, L1_gnn_u5_b):
    import numpy as np
    import concourse.bacc as bacc
    from concourse import mybir
    from concourse.bass_utils import run_bass_kernel_spmd

    def turned(a):
        return np.ascontiguousarray(np.asarray(a).T)

    def column(a):
        return np.ascontiguousarray(np.asarray(a).reshape(-1, 128).T)

    arrays = {
        "x": np.ascontiguousarray(x), "adj": np.ascontiguousarray(adj), "adj_t": turned(adj),
        "wq": np.ascontiguousarray(L0_gnn_Wq), "wk": np.ascontiguousarray(L0_gnn_Wk), "wv_t": turned(L0_gnn_Wv),
        "w3_t": turned(L1_gnn_w3_w), "b3": column(L1_gnn_w3_b), "u3_t": turned(L1_gnn_u3_w), "bu3": column(L1_gnn_u3_b),
        "w4_t": turned(L1_gnn_w4_w), "b4": column(L1_gnn_w4_b), "w5_t": turned(L1_gnn_w5_w), "b5": column(L1_gnn_w5_b),
        "u5_t": turned(L1_gnn_u5_w), "bu5": column(L1_gnn_u5_b),
    }
    nc = bacc.Bacc("TRN2", target_bir_lowering=False, num_devices=1)
    args = {n: nc.dram_tensor(n, a.shape, mybir.dt.from_np(a.dtype), kind="ExternalInput").ap()
            for n, a in arrays.items()}
    out = nc.dram_tensor("out", x.shape, mybir.dt.float32, kind="ExternalOutput").ap()
    gated_graph_kernel(nc, *args.values(), out)
    r = run_bass_kernel_spmd(nc, [arrays], core_ids=[0])
    return r.results[0]["out"]
```

```python
import concourse.bass as bass
from concourse import mybir
from contextlib import ExitStack



def gated_graph_kernel(nc, x, adj, adj_t, wq, wk, wv_t, w3_t, b3, u3_t, bu3, w4_t, b4, w5_t, b5,
                       u5_t, bu5, out):
    f32 = mybir.dt.float32
    f32r = mybir.dt.float32r
    ALU = mybir.AluOpType
    ACT = mybir.ActivationFunctionType

    P = 128
    B, N, D = x.shape
    C = D // P
    Q = 4
    T = Q * P
    G = B * N // T
    PAIRS = G // 2
    EPS = 1e-5

    x_g = x.rearrange("b n d -> (b n) d").rearrange("(g q p) d -> g p q d", q=Q, p=P)
    out_g = out.rearrange("b n d -> (b n) d").rearrange("(g q p) d -> g p q d", q=Q, p=P)

    TOK_START = ["split x 0", "v 0", "split x 1", "sum 0", "v 1", "new first", "adj' first", "sum 1",
                 "new 0", "adj' 0"]
    TOK_ROUND = ["step 1", "adj' 1", "split x X", "step 2", "adj' 2", "v X", "sum X", "step 3",
                 "adj' 3", "split x Y", "step 4", "adj' 4", "v Y", "sum Y", "final 5", "new 5",
                 "adj' 5", "final 0", "new 0", "adj' 0"]
    TOK_END = ["step 1", "adj' 1", "step 2", "adj' 2", "step 3", "adj' 3", "step 4", "adj' 4",
               "final 5", "final 0"]
    FEA_START = ["q 0", "rel 0", "norm 0", "q 1", "rel 1", "adj first", "norm 1", "adj 0"]
    FEA_ROUND = ["adj 1", "q X", "adj 2", "rel X", "norm X", "adj 3", "q Y", "adj 4", "rel Y",
                 "norm Y", "adj 5", "adj 0"]
    FEA_END = ["adj 1", "adj 2", "adj 3", "adj 4"]

    def use_in_start(name):
        names = TOK_START if name in TOK_START else FEA_START
        return names.index(name)

    def use_in_round(name, i):
        names, first = (TOK_ROUND, len(TOK_START)) if name in TOK_ROUND else (FEA_ROUND, len(FEA_START))
        return i * len(names) + (first + names.index(name))

    def use_in_end(name):
        if name in TOK_END:
            return len(TOK_START) + (PAIRS - 1) * len(TOK_ROUND) + TOK_END.index(name)
        return len(FEA_START) + (PAIRS - 1) * len(FEA_ROUND) + FEA_END.index(name)

    ctx = ExitStack()
    with ctx:
        def sb(name, shape, dt=f32):
            return ctx.enter_context(nc.sbuf_tensor(name, shape, dt))

        def sem(name):
            return ctx.enter_context(nc.semaphore(name))

        names = ("m", "v", "u3", "w4", "wz", "w5", "u5")
        W_hi = {n: sb(f"W_hi_{n}", [P, C, D], f32r) for n in names}
        W_lo = {n: sb(f"W_lo_{n}", [P, C, D], f32r) for n in names}
        adjT = sb("adjT", [P, P])
        adjT_s = sb("adjT_s", [P, 2, P], f32r)
        adjT_hi, adjT_lo = adjT_s[:, 0, :], adjT_s[:, 1, :]
        mask = sb("mask", [P, Q, P])
        ident = sb("ident", [P, P])
        ones = sb("ones", [P, 1])
        fence = sb("fence", [P, 4])
        minus_half = sb("minus_half", [P, Q])
        b_in = sb("b_in", [P, 5, C])
        b_r = sb("b_r", [P, C])
        b_z = sb("b_z", [P, C])
        b_c = sb("b_c", [P, C])

        x_s = [sb(f"x_s{s}", [P, Q, D]) for s in range(2)]
        resid = [sb(f"resid{s}", [P, Q, D]) for s in range(2)]
        h0 = [sb(f"h0{s}", [P, Q, D]) for s in range(2)]
        h = [sb(f"h{s}", [P, C, T]) for s in range(2)]
        h_hi = [sb(f"h_hi{s}", [P, C, T], f32r) for s in range(2)]
        h_lo = [sb(f"h_lo{s}", [P, C, T], f32r) for s in range(2)]
        a_hi = [sb(f"a_hi{s}", [P, C, T], f32r) for s in range(2)]
        a_lo = [sb(f"a_lo{s}", [P, C, T], f32r) for s in range(2)]
        o_s = [sb(f"o_s{s}", [P, Q, D]) for s in range(2)]

        t_hi = sb("t_hi", [P, Q, D], f32r)
        t_lo = sb("t_lo", [P, Q, D], f32r)
        r_s = sb("r_s", [P, C, T])
        z_s = sb("z_s", [P, C, T])
        c_s = sb("c_s", [P, C, T])
        d_s = sb("d_s", [P, C, T])
        a_aside = sb("a_aside", [P, C, T])
        a_s = sb("a_s", [P, C, T])
        rh = sb("rh", [P, C, T])
        rh_hi = sb("rh_hi", [P, C, T], f32r)
        rh_lo = sb("rh_lo", [P, C, T], f32r)

        hx = sb("hx", [P, Q, D])
        hxT_hi = sb("hxT_hi", [P, C, T], f32r)
        hxT_lo = sb("hxT_lo", [P, C, T], f32r)
        q_s = sb("q_s", [P, 2, C, T], f32r)
        q_hi, q_lo = q_s[:, 0, :, :], q_s[:, 1, :, :]
        v_hi = sb("v_hi", [P, Q, D], f32r)
        v_lo = sb("v_lo", [P, Q, D], f32r)
        S = sb("S", [P, Q, P])
        S_hi = sb("S_hi", [P, Q, P], f32r)
        S_lo = sb("S_lo", [P, Q, P], f32r)
        S_sum = sb("S_sum", [P, Q, P])
        S_aside = sb("S_aside", [P, Q, P])
        sq = sb("sq", [P, Q, P])
        bn = [sb(f"bn{n}", [P, Q, 6]) for n in range(2)]
        mv = [sb(f"mv{n}", [P, Q, 2]) for n in range(2)]
        vare = [sb(f"vare{n}", [P, Q]) for n in range(2)]
        rstd = [sb(f"rstd{n}", [P, Q]) for n in range(2)]
        shift = [sb(f"shift{n}", [P, Q]) for n in range(2)]
        norm2 = sb("norm2", [P, Q])
        rnorm = sb("rnorm", [P, Q])

        raw = {"w3": r_s, "w4": z_s, "w5": c_s}
        raw["u3"], raw["u5"] = rh[:, 0, :], rh[:, 1, :]
        raw["q"], raw["k"] = d_s[:, 0, :], d_s[:, 1, :]
        raw["v"] = o_s[0][:, 0:2, :].rearrange("p a b -> p (a b)")
        sum4 = o_s[0][:, 2:4, :].rearrange("p a b -> p (a b)")
        sumz = o_s[1][:, 0:2, :].rearrange("p a b -> p (a b)")
        sum5 = o_s[1][:, 2:4, :].rearrange("p a b -> p (a b)")

        gate = ctx.enter_context(nc.psum_tensor("gate", [P, C, T], f32))
        cand = ctx.enter_context(nc.psum_tensor("cand", [P, C, T], f32))
        tok = ctx.enter_context(nc.psum_tensor("tok", [P, Q, D], f32))
        fea = ctx.enter_context(nc.psum_tensor("fea", [P, C, T], f32))
        tokT = tok[:].rearrange("p (c a) d -> p c (a d)", c=C)
        tokA = tok[:].rearrange("p q (h n) -> p q h n", h=2)
        feaA = fea[:].rearrange("p c (a h n) -> p (c a) h n", h=2, n=P)
        HQ = Q // 2

        attn_w_in, adj_in, gate_w_in, bias_in = sem("attn_w_in"), sem("adj_in"), sem("gate_w_in"), sem("bias_in")
        x_in = [sem("x_in0"), sem("x_in1")]
        stored = [sem("stored0"), sem("stored1")]
        const_zero, const_ready = sem("const_zero"), sem("const_ready")
        sum3_ready = sem("sum3_ready")
        m_full, w_sum, w_hi_ready, w_lo_ready, bias_ready = (
            sem("m_full"), sem("w_sum"), sem("w_hi_ready"), sem("w_lo_ready"), sem("bias_ready"))
        tok_full, tok_taken, fea_full, fea_taken = sem("tok_full"), sem("tok_taken"), sem("fea_full"), sem("fea_taken")
        r_full, z_full, c_full = sem("r_full"), sem("z_full"), sem("c_full")
        r_ready, z_ready, c_ready = sem("r_ready"), sem("z_ready"), sem("c_ready")
        rh_ready, rh_hi_ready, rh_lo_ready = sem("rh_ready"), sem("rh_hi_ready"), sem("rh_lo_ready")
        diff_ready, prod_ready, upd_ready = sem("diff_ready"), sem("prod_ready"), sem("upd_ready")
        h_hi_ready, t_hi_ready, a_hi_ready = sem("h_hi_ready"), sem("t_hi_ready"), sem("a_hi_ready")
        a_aside_ready, a_lo_ready = sem("a_aside_ready"), sem("a_lo_ready")
        h_lo_ready = sem("h_lo_ready")
        h_new_ready = sem("h_new_ready")
        t_lo_ready = sem("t_lo_ready")
        resid_ready = sem("resid_ready")
        bn_ready = [sem("bn_ready0"), sem("bn_ready1")]
        mv_ready = [sem("mv_ready0"), sem("mv_ready1")]
        vare_ready = [sem("vare_ready0"), sem("vare_ready1")]
        rstd_ready = [sem("rstd_ready0"), sem("rstd_ready1")]
        shift_ready = [sem("shift_ready0"), sem("shift_ready1")]
        hx_ready, h0_ready = sem("hx_ready"), sem("h0_ready")
        hxT_hi_ready, q_hi_ready, v_hi_ready = sem("hxT_hi_ready"), sem("q_hi_ready"), sem("v_hi_ready")
        S_aside_ready, S_ready, S_hi_ready, S_lo_ready = (
            sem("S_aside_ready"), sem("S_ready"), sem("S_hi_ready"), sem("S_lo_ready"))
        sq_ready = sem("sq_ready")
        rnorm_ready = sem("rnorm_ready")
        fence_done = [sem(f"fence_done{n}") for n in range(3)]

        block = ctx.enter_context(nc.Block())

        def graph_pair(q):
            return slice(q * P, (q + 1) * P)

        @block.sync
        def _(sp):
            def load_x(g, s):
                sp.dma_start(x_s[s][:], x_g[g]).then_inc(x_in[s], 16)

            def store(g, s, n_final):
                sp.wait_ge(tok_taken, 2 * n_final + 2)
                sp.dma_start(out_g[g], o_s[s][:]).then_inc(stored[s], 16)

            for s in range(2):
                sp.sem_inc(stored[s], 16)
            load_x(0, 0)
            sp.dma_start(raw["q"].rearrange("p (c n) -> p c n", c=C),
                         wq.rearrange("(c p) n -> p c n", p=P)).then_inc(attn_w_in, 16)
            sp.dma_start(raw["k"].rearrange("p (c n) -> p c n", c=C),
                         wk.rearrange("(c p) n -> p c n", p=P)).then_inc(attn_w_in, 16)
            sp.dma_start(raw["v"].rearrange("p (c n) -> p c n", c=C),
                         wv_t.rearrange("(c p) n -> p c n", p=P)).then_inc(attn_w_in, 16)
            load_x(1, 1)
            sp.wait_ge(const_zero, 1)
            for e in range(2):
                part = slice(e * N, (e + 1) * N)
                sp.dma_start(adjT[part, part], adj_t).then_inc(adj_in, 16)
                for q in range(Q):
                    sp.dma_start(mask[part, q, part], adj).then_inc(adj_in, 16)
            for name, src in (("w4", w4_t), ("w3", w3_t), ("w5", w5_t)):
                sp.dma_start(raw[name][:].rearrange("p a (c n) -> p (a c) n", n=D),
                             src.rearrange("(c p) n -> p c n", p=P)).then_inc(gate_w_in, 16)
            for name, src in (("u3", u3_t), ("u5", u5_t)):
                sp.dma_start(raw[name].rearrange("p (c n) -> p c n", c=C),
                             src.rearrange("(c p) n -> p c n", p=P)).then_inc(gate_w_in, 16)
            for n, src in enumerate((b3, bu3, b4, b5, bu5)):
                sp.dma_start(b_in[:, n, :], src).then_inc(bias_in, 16)

            with sp.Fori(0, PAIRS - 1) as i:
                for s in range(2):
                    sp.wait_ge(resid_ready, 2 * i + (s + 1))
                    load_x(2 * i + 2 + s, s)
                store(2 * i, 0, use_in_round("final 5", i))
                store(2 * i + 1, 1, use_in_round("final 0", i))
            store(G - 2, 0, use_in_end("final 5"))
            store(G - 1, 1, use_in_end("final 0"))
            for s in range(2):
                sp.wait_ge(stored[s], 16 * PAIRS + 16)

        @block.gpsimd
        def _(pool):
            nc.gpsimd.memset(adjT[:], 0.0)
            nc.gpsimd.memset(mask[:], 0.0).then_inc(const_zero, 1)
            nc.gpsimd.memset(ones[:], 1.0)
            nc.gpsimd.memset(minus_half[:], -0.5)
            nc.gpsimd.memset(ident[:], 0.0).then_inc(const_zero, 1)
            pool.wait_ge(const_zero, 2)
            nc.gpsimd.affine_select(out=ident[:], in_=ident[:], compare_op=ALU.not_equal, fill=1.0,
                                    base=0, pattern=[[-1, P]], channel_multiplier=1).then_inc(const_ready, 1)

            def inverse_std(n, g):
                pool.wait_ge(vare_ready[n], g + 1)
                nc.gpsimd.tensor_tensor(rstd[n][:], vare[n][:], minus_half[:], ALU.pow).then_inc(rstd_ready[n], 1)

            def inverse_norm(n):
                pool.wait_ge(fea_taken, 2 * n + 2)
                nc.gpsimd.tensor_tensor(rnorm[:], norm2[:], minus_half[:], ALU.pow).then_inc(rnorm_ready, 1)

            def keep_resid(g, s, n_final):
                pool.wait_ge(h0_ready, Q * (g + 1))
                if n_final is not None:
                    pool.wait_ge(tok_taken, 2 * n_final + 2)
                pool.wait_ge(fence_done[2], g)
                nc.gpsimd.tensor_tensor(fence[:, 2:3], ones[:], ones[:], ALU.mult).then_inc(fence_done[2], 1)
                nc.gpsimd.tensor_copy(resid[s][:], x_s[s][:]).then_inc(resid_ready, 1)

            n = use_in_start
            inverse_std(0, 0)
            inverse_std(0, 1)
            inverse_norm(n("norm 0"))
            inverse_std(1, 0)
            inverse_norm(n("norm 1"))
            keep_resid(0, 0, None)
            inverse_std(1, 1)
            keep_resid(1, 1, None)
            with pool.Fori(0, PAIRS - 1) as i:
                inverse_std(0, 2 * i + 2)
                inverse_std(0, 2 * i + 3)
                inverse_norm(use_in_round("norm X", i))
                inverse_std(1, 2 * i + 2)
                inverse_norm(use_in_round("norm Y", i))
                inverse_std(1, 2 * i + 3)
                keep_resid(2 * i + 2, 0, use_in_round("final 5", i))
                keep_resid(2 * i + 3, 1, use_in_round("final 0", i))

        @block.tensor
        def _(pe):
            def product(dst, lhs, rhs, start, stop):
                (l_hi, l_lo), (r_hi, r_lo) = lhs, rhs
                nc.tensor.matmul(dst, l_hi, r_hi, start=start, stop=False, skip_group_check=True)
                nc.tensor.matmul(dst, l_hi, r_lo, start=False, stop=False, skip_group_check=True)
                return nc.tensor.matmul(dst, l_lo, r_hi, start=False, stop=stop, skip_group_check=True)

            def weight(n, c, o):
                return W_hi[n][:, c, o * P:(o + 1) * P], W_lo[n][:, c, o * P:(o + 1) * P]

            def linear(dst, n, o, hi, lo, start, stop):
                for c in range(C):
                    last = product(dst, weight(n, c, o), (hi[:, c, :], lo[:, c, :]),
                                   start and c == 0, stop and c == C - 1)
                return last

            def tok_wait(n, b):
                if isinstance(n, int) and n == 0:
                    return
                pe.wait_ge(tok_taken, 2 * n + (b - 1))

            def fea_wait(n, b):
                if isinstance(n, int) and n == 0:
                    return
                pe.wait_ge(fea_taken, 2 * n + (b - 1))

            def transpose_hx(g, n):
                pe.wait_ge(hx_ready, Q * (g + 1))
                for c in range(C):
                    tok_wait(n, c)
                    for q in range(Q):
                        last = nc.tensor.transpose(tokT[:, c, graph_pair(q)], hx[:, q, c * P:(c + 1) * P], ident[:])
                    last.then_inc(tok_full, 1)

            def queries(g, n, n_hx):
                pe.wait_ge(hxT_hi_ready, 2 * g + 2)
                pe.wait_ge(tok_taken, 2 * n_hx + 2)
                for c in range(C):
                    fea_wait(n, c)
                    linear(fea[:, c, :], "m", c, hxT_hi, hxT_lo, True, True).then_inc(fea_full, 1)

            def values(g, n):
                for b in range(2):
                    tok_wait(n, b)
                    for q in range(HQ * b, HQ * b + HQ):
                        for c in range(C):
                            last = product(tok[:, q, :], (hxT_hi[:, c, graph_pair(q)], hxT_lo[:, c, graph_pair(q)]),
                                           (W_hi["v"][:, c, :], W_lo["v"][:, c, :]), c == 0, c == C - 1)
                    last.then_inc(tok_full, 1)

            def scores(g, n, n_q):
                pe.wait_ge(q_hi_ready, 2 * g + 2)
                pe.wait_ge(fea_taken, 2 * n_q + 2)
                fea_wait(n, 0)
                fea_wait(n, 1)
                for q in range(Q):
                    for c in range(C):
                        nc.tensor.matmul(feaA[:, q, :, :], hxT_hi[:, c, graph_pair(q)], q_s[:, :, c, graph_pair(q)],
                                         start=c == 0, stop=False, skip_group_check=True)
                        last = nc.tensor.matmul(feaA[:, q, 0, :], hxT_lo[:, c, graph_pair(q)], q_hi[:, c, graph_pair(q)],
                                                start=False, stop=c == C - 1, skip_group_check=True)
                last.then_inc(fea_full, 2)

            def norms(g, n_fea):
                pe.wait_ge(sq_ready, g + 1)
                fea_wait(n_fea, 1)
                for q in range(Q):
                    last = nc.tensor.matmul(fea[:, 1, q:q + 1], sq[:, q, :], ones[:], start=True, stop=True)
                last.then_inc(fea_full, 2)

            def weighted_sum(g, n_tok, n_v):
                pe.wait_ge(S_hi_ready, g + 1)
                pe.wait_ge(S_lo_ready, g + 1)
                pe.wait_ge(v_hi_ready, 2 * g + 2)
                pe.wait_ge(tok_taken, 2 * n_v + 2)
                for b in range(2):
                    tok_wait(n_tok, b)
                    for q in range(HQ * b, HQ * b + HQ):
                        last = product(tok[:, q, :], (S_hi[:, q, :], S_lo[:, q, :]),
                                       (v_hi[:, q, :], v_lo[:, q, :]), True, True)
                    last.then_inc(tok_full, 1)

            def transpose_state(w, o, n):
                pe.wait_ge(upd_ready, 2 * w)
                for b in range(2):
                    tok_wait(n, b)
                    for q in range(HQ * b, HQ * b + HQ):
                        for c in range(C):
                            last = nc.tensor.transpose(tok[:, q, c * P:(c + 1) * P], h[o][:, c, graph_pair(q)], ident[:])
                    last.then_inc(tok_full, 1)

            def adjacency(v, c, banks, n):
                pe.wait_ge(t_hi_ready, 2 * v + 2)
                wait, full = (fea_wait, fea_full) if banks is feaA else (tok_wait, tok_full)
                wait(n, 0)
                wait(n, 1)
                for q in range(Q):
                    nc.tensor.matmul(banks[:, q, :, :], t_hi[:, q, c * P:(c + 1) * P], adjT_s[:],
                                     start=True, stop=False, skip_group_check=True)
                    last = nc.tensor.matmul(banks[:, q, 0, :], t_lo[:, q, c * P:(c + 1) * P], adjT_hi,
                                            start=False, stop=True, skip_group_check=True)
                last.then_inc(full, 2)

            def transpose_new(g, s, n):
                for c in range(C):
                    tok_wait(n, c)
                    for q in range(Q):
                        last = nc.tensor.transpose(tokT[:, c, graph_pair(q)], h0[s][:, q, c * P:(c + 1) * P], ident[:])
                    last.then_inc(tok_full, 1)

            def reset_gate(w, s):
                pe.wait_ge(h_hi_ready, 2 * w + 2)
                for o in range(C):
                    if not (isinstance(w, int) and w == 0):
                        pe.wait_ge(z_ready, 2 * w + (o - 1))
                    linear(gate[:, o, :], "u3", o, h_hi[s], h_lo[s], True, False)
                pe.wait_ge(a_hi_ready, 2 * w + 2)
                pe.wait_ge(a_lo_ready, 2 * w + 2)
                for o in range(C):
                    linear(gate[:, o, :], "w4", o, a_hi[s], a_lo[s], False, True).then_inc(r_full, 1)

            def update_gate(w, s):
                if isinstance(w, int) and w == 0:
                    pe.wait_ge(w_lo_ready, 6)
                for o in range(C):
                    pe.wait_ge(r_ready, 2 * w + (o + 1))
                    linear(gate[:, o, :], "wz", o, a_hi[s], a_lo[s], False, True).then_inc(z_full, 1)

            def candidate_a(w, s):
                if isinstance(w, int) and w == 0:
                    pe.wait_ge(w_lo_ready, 7)
                for o in range(C):
                    if not (isinstance(w, int) and w == 0):
                        pe.wait_ge(c_ready, 2 * w + (o - 1))
                    linear(cand[:, o, :], "w5", o, a_hi[s], a_lo[s], True, False)

            def candidate_rh(w, s):
                if isinstance(w, int) and w == 0:
                    pe.wait_ge(w_lo_ready, len(names) + 1)
                pe.wait_ge(rh_hi_ready, 2 * w + 2)
                pe.wait_ge(rh_lo_ready, 2 * w + 2)
                for o in range(C):
                    linear(cand[:, o, :], "u5", o, rh_hi, rh_lo, False, True).then_inc(c_full, 1)

            def window(i, k, use, attention=True, new=True):
                w, s, o = 6 * i + k, k % 2, 1 - k % 2
                if k == 1:
                    pe.wait_ge(tok_taken, 2 * use_in_round("new 0", i - 1) + 2)
                    reset_gate(w, s)
                    transpose_state(w, o, use("step 1"))
                    update_gate(w, s)
                    pe.wait_ge(tok_taken, 2 * use("step 1") + 2)
                    adjacency(w + 1, 0, feaA, use("adj 1"))
                    candidate_a(w, s)
                    adjacency(w + 1, 1, tokA, use("adj' 1"))
                    candidate_rh(w, s)
                    if attention:
                        transpose_hx(2 * i + 2, use("split x X"))
                elif k == 2:
                    pe.wait_ge(h_lo_ready, 8 * i + 2)
                    reset_gate(w, s)
                    if attention:
                        queries(2 * i + 2, use("q X"), use("split x X"))
                    transpose_state(w, o, use("step 2"))
                    update_gate(w, s)
                    pe.wait_ge(tok_taken, 2 * use("step 2") + 2)
                    adjacency(w + 1, 0, feaA, use("adj 2"))
                    adjacency(w + 1, 1, tokA, use("adj' 2"))
                    if attention:
                        scores(2 * i + 2, use("rel X"), use("q X"))
                    candidate_a(w, s)
                    if attention:
                        values(2 * i + 2, use("v X"))
                        norms(2 * i + 2, use("norm X"))
                    candidate_rh(w, s)
                elif k == 3:
                    if attention:
                        weighted_sum(2 * i + 2, use("sum X"), use("v X"))
                    pe.wait_ge(h_lo_ready, 8 * i + 4)
                    reset_gate(w, s)
                    transpose_state(w, o, use("step 3"))
                    update_gate(w, s)
                    pe.wait_ge(tok_taken, 2 * use("step 3") + 2)
                    adjacency(w + 1, 0, feaA, use("adj 3"))
                    adjacency(w + 1, 1, tokA, use("adj' 3"))
                    candidate_a(w, s)
                    if attention:
                        transpose_hx(2 * i + 3, use("split x Y"))
                    candidate_rh(w, s)
                    if attention:
                        queries(2 * i + 3, use("q Y"), use("split x Y"))
                elif k == 4:
                    pe.wait_ge(h_lo_ready, 8 * i + 6)
                    reset_gate(w, s)
                    transpose_state(w, o, use("step 4"))
                    update_gate(w, s)
                    pe.wait_ge(tok_taken, 2 * use("step 4") + 2)
                    adjacency(w + 1, 0, feaA, use("adj 4"))
                    adjacency(w + 1, 1, tokA, use("adj' 4"))
                    candidate_a(w, s)
                    if attention:
                        scores(2 * i + 3, use("rel Y"), use("q Y"))
                        values(2 * i + 3, use("v Y"))
                    candidate_rh(w, s)
                    if attention:
                        norms(2 * i + 3, use("norm Y"))
                elif k == 5:
                    if attention:
                        weighted_sum(2 * i + 3, use("sum Y"), use("v Y"))
                    pe.wait_ge(h_lo_ready, 8 * i + 8)
                    reset_gate(w, s)
                    transpose_state(w, o, use("final 5"))
                    update_gate(w, s)
                    if new:
                        pe.wait_ge(t_lo_ready, 4 * i + 6)
                        transpose_new(2 * i + 2, o, use("new 5"))
                        adjacency(w + 1, 0, feaA, use("adj 5"))
                    candidate_a(w, s)
                    if new:
                        adjacency(w + 1, 1, tokA, use("adj' 5"))
                    candidate_rh(w, s)
                else:
                    pe.wait_ge(tok_taken, 2 * use("new 5") + 2)
                    reset_gate(w, s)
                    transpose_state(w, o, use("final 0"))
                    update_gate(w, s)
                    pe.wait_ge(t_lo_ready, 4 * i + 4)
                    transpose_new(2 * i + 1, o, use("new 0"))
                    adjacency(w + 1, 0, feaA, use("adj 0"))
                    candidate_a(w, s)
                    adjacency(w + 1, 1, tokA, use("adj' 0"))
                    candidate_rh(w, s)

            pe.wait_ge(attn_w_in, 48)
            for c in range(C):
                for e in range(C):
                    last = nc.tensor.matmul(gate[:, 0, c * D:(c + 1) * D], raw["q"][:, e * D + c * P:e * D + (c + 1) * P],
                                            raw["k"][:, e * D:(e + 1) * D], start=e == 0, stop=e == C - 1)
            last.then_inc(m_full, 1)
            pe.wait_ge(const_ready, 1)
            n = use_in_start
            transpose_hx(0, n("split x 0"))
            pe.wait_ge(w_lo_ready, 1)
            queries(0, n("q 0"), n("split x 0"))
            pe.wait_ge(w_lo_ready, 2)
            values(0, n("v 0"))
            scores(0, n("rel 0"), n("q 0"))
            transpose_hx(1, n("split x 1"))
            norms(0, n("norm 0"))
            weighted_sum(0, n("sum 0"), n("v 0"))
            queries(1, n("q 1"), n("split x 1"))
            values(1, n("v 1"))
            scores(1, n("rel 1"), n("q 1"))
            pe.wait_ge(w_lo_ready, 3)
            pe.wait_ge(t_lo_ready, 2)
            transpose_new(0, 0, n("new first"))
            adjacency(0, 0, feaA, n("adj first"))
            adjacency(0, 1, tokA, n("adj' first"))
            pe.wait_ge(w_lo_ready, 5)
            norms(1, n("norm 1"))
            weighted_sum(1, n("sum 1"), n("v 1"))
            pe.wait_ge(tok_taken, 2 * n("new first") + 2)
            reset_gate(0, 0)
            update_gate(0, 0)
            candidate_a(0, 0)
            pe.wait_ge(t_lo_ready, 4)
            transpose_new(1, 1, n("new 0"))
            adjacency(1, 0, feaA, n("adj 0"))
            candidate_rh(0, 0)
            adjacency(1, 1, tokA, n("adj' 0"))
            with pe.Fori(0, PAIRS - 1) as i:
                for k in (1, 2, 3, 4, 5):
                    window(i, k, lambda name: use_in_round(name, i))
                window(i + 1, 0, lambda name: use_in_round(name, i))
            for k in (1, 2, 3, 4):
                window(PAIRS - 1, k, use_in_end, attention=False)
            window(PAIRS - 1, 5, use_in_end, attention=False, new=False)
            transpose_state(6 * PAIRS, 1, use_in_end("final 0"))

        @block.scalar
        def _(act):
            def copy(dst, src):
                return nc.scalar.activation(dst, src, ACT.Copy)

            def tok_wait(n, b):
                act.wait_ge(tok_full, 2 * n + (b + 1))

            def fea_wait(n, b):
                act.wait_ge(fea_full, 2 * n + (b + 1))

            def split_weight(n, name, src):
                act.wait_ge(w_sum, n)
                copy(W_hi[name][:].rearrange("p c n -> p (c n)"), src).then_inc(w_hi_ready, 1)

            def normalise(n, g, s):
                act.wait_ge(shift_ready[n], g + 1)
                dst, done = (hx, hx_ready) if n == 0 else (h0[s], h0_ready)
                for q in range(Q):
                    nc.scalar.activation(dst[:, q, :], x_s[s][:, q, :], ACT.Relu, bias=shift[n][:, q:q + 1],
                                         scale=rstd[n][:, q:q + 1]).then_inc(done, 1)

            def split_hx(n):
                for c in range(C):
                    tok_wait(n, c)
                    copy(hxT_hi[:, c, :], tokT[:, c, :]).then_inc(hxT_hi_ready, 1)

            def split_q(n):
                for c in range(C):
                    fea_wait(n, c)
                    copy(q_hi[:, c, :], fea[:, c, :]).then_inc(q_hi_ready, 1)

            def split_v(n):
                for b in range(2):
                    tok_wait(n, b)
                    copy(v_hi[:, HQ * b:HQ * b + HQ, :], tok[:, HQ * b:HQ * b + HQ, :]).then_inc(v_hi_ready, 1)

            def take_S_aside(n):
                fea_wait(n, 1)
                copy(S_aside[:], feaA[:, :, 1, :]).then_inc(S_aside_ready, 1)

            def split_S(g):
                act.wait_ge(S_ready, g + 1)
                copy(S_hi[:], S[:]).then_inc(S_hi_ready, 1)
                nc.scalar.activation(sq[:], S[:], ACT.Square).then_inc(sq_ready, 1)

            def split_state(w, o):
                for c in range(C):
                    act.wait_ge(upd_ready, 2 * w + (c - 1))
                    copy(h_hi[o][:, c, :], h[o][:, c, :]).then_inc(h_hi_ready, 1)

            def split_tok(n):
                for b in range(2):
                    tok_wait(n, b)
                    copy(t_hi[:, HQ * b:HQ * b + HQ, :], tok[:, HQ * b:HQ * b + HQ, :]).then_inc(t_hi_ready, 1)

            def split_h0(g, s):
                for b in range(2):
                    act.wait_ge(h0_ready, Q * g + HQ * (b + 1))
                    copy(t_hi[:, HQ * b:HQ * b + HQ, :], h0[s][:, HQ * b:HQ * b + HQ, :]).then_inc(t_hi_ready, 1)

            def take_a_aside(c, banks, n):
                (fea_wait if banks is feaA else tok_wait)(n, 1)
                copy(a_aside[:, c, :].rearrange("p (q n) -> p q n", q=Q), banks[:, :, 1, :]).then_inc(a_aside_ready, 1)

            def split_a(s, c, banks, n):
                act.wait_ge(fea_taken if banks is feaA else tok_taken, 2 * n + 2)
                copy(a_hi[s][:, c, :], a_s[:, c, :]).then_inc(a_hi_ready, 1)

            def split_new(s, n):
                for c in range(C):
                    tok_wait(n, c)
                    copy(h_hi[s][:, c, :], tokT[:, c, :]).then_inc(h_hi_ready, 1)

            def reset_sigmoid(w):
                for c in range(C):
                    act.wait_ge(r_full, 2 * w + (c + 1))
                    nc.scalar.activation(r_s[:, c, :], gate[:, c, :], ACT.Sigmoid,
                                         bias=b_r[:, c:c + 1]).then_inc(r_ready, 1)

            def split_rh(w):
                for c in range(C):
                    act.wait_ge(rh_ready, 2 * w + (c + 1))
                    copy(rh_hi[:, c, :], rh[:, c, :]).then_inc(rh_hi_ready, 1)

            def update_sigmoid(w):
                if not (isinstance(w, int) and w == 0):
                    act.wait_ge(upd_ready, 2 * w)
                for c in range(C):
                    act.wait_ge(z_full, 2 * w + (c + 1))
                    nc.scalar.activation(z_s[:, c, :], gate[:, c, :], ACT.Sigmoid,
                                         bias=b_z[:, c:c + 1]).then_inc(z_ready, 1)

            def candidate_tanh(w):
                for c in range(C):
                    act.wait_ge(c_full, 2 * w + (c + 1))
                    nc.scalar.activation(c_s[:, c, :], cand[:, c, :], ACT.Tanh,
                                         bias=b_c[:, c:c + 1]).then_inc(c_ready, 1)

            def window(i, k, use, attention=True, new=True):
                w, s, o = 6 * i + k, k % 2, 1 - k % 2
                if k == 1:
                    split_state(w, o)
                    reset_sigmoid(w)
                    split_tok(use("step 1"))
                    update_sigmoid(w)
                    take_a_aside(0, feaA, use("adj 1"))
                    split_rh(w)
                    if attention:
                        normalise(0, 2 * i + 2, 0)
                    take_a_aside(1, tokA, use("adj' 1"))
                    split_a(o, 0, feaA, use("adj 1"))
                    split_a(o, 1, tokA, use("adj' 1"))
                    candidate_tanh(w)
                    if attention:
                        split_hx(use("split x X"))
                elif k == 2:
                    split_state(w, o)
                    reset_sigmoid(w)
                    if attention:
                        split_q(use("q X"))
                    split_tok(use("step 2"))
                    take_a_aside(0, feaA, use("adj 2"))
                    split_rh(w)
                    split_a(o, 0, feaA, use("adj 2"))
                    take_a_aside(1, tokA, use("adj' 2"))
                    split_a(o, 1, tokA, use("adj' 2"))
                    if attention:
                        take_S_aside(use("rel X"))
                        split_S(2 * i + 2)
                        split_v(use("v X"))
                    update_sigmoid(w)
                    candidate_tanh(w)
                elif k == 3:
                    split_state(w, o)
                    reset_sigmoid(w)
                    split_tok(use("step 3"))
                    if attention:
                        normalise(0, 2 * i + 3, 1)
                    split_rh(w)
                    take_a_aside(0, feaA, use("adj 3"))
                    take_a_aside(1, tokA, use("adj' 3"))
                    split_a(o, 0, feaA, use("adj 3"))
                    update_sigmoid(w)
                    split_a(o, 1, tokA, use("adj' 3"))
                    if attention:
                        split_hx(use("split x Y"))
                        normalise(1, 2 * i + 2, 0)
                    candidate_tanh(w)
                elif k == 4:
                    if attention:
                        split_q(use("q Y"))
                    split_state(w, o)
                    reset_sigmoid(w)
                    split_tok(use("step 4"))
                    take_a_aside(0, feaA, use("adj 4"))
                    split_rh(w)
                    update_sigmoid(w)
                    take_a_aside(1, tokA, use("adj' 4"))
                    split_a(o, 0, feaA, use("adj 4"))
                    split_a(o, 1, tokA, use("adj' 4"))
                    if attention:
                        take_S_aside(use("rel Y"))
                        split_S(2 * i + 3)
                        split_v(use("v Y"))
                    candidate_tanh(w)
                elif k == 5:
                    if new:
                        split_h0(2 * i + 2, o)
                    reset_sigmoid(w)
                    split_rh(w)
                    if new:
                        split_new(o, use("new 5"))
                    update_sigmoid(w)
                    if new:
                        take_a_aside(0, feaA, use("adj 5"))
                        take_a_aside(1, tokA, use("adj' 5"))
                        split_a(o, 0, feaA, use("adj 5"))
                        split_a(o, 1, tokA, use("adj' 5"))
                    candidate_tanh(w)
                    if attention:
                        normalise(1, 2 * i + 3, 1)
                else:
                    split_h0(2 * i + 1, o)
                    reset_sigmoid(w)
                    split_rh(w)
                    split_new(o, use("new 0"))
                    take_a_aside(0, feaA, use("adj 0"))
                    update_sigmoid(w)
                    split_a(o, 0, feaA, use("adj 0"))
                    take_a_aside(1, tokA, use("adj' 0"))
                    split_a(o, 1, tokA, use("adj' 0"))
                    candidate_tanh(w)

            n = use_in_start
            act.wait_ge(const_zero, 2)
            nc.scalar.activation(fence[:, 3:4], ones[:], ACT.Sigmoid)
            normalise(0, 0, 0)
            act.wait_ge(m_full, 1)
            split_weight(0, "m", gate[:, 0, :])
            split_hx(n("split x 0"))
            act.wait_ge(attn_w_in, 48)
            split_weight(0, "v", raw["v"])
            split_q(n("q 0"))
            normalise(0, 1, 1)
            split_v(n("v 0"))
            take_S_aside(n("rel 0"))
            split_S(0)
            split_hx(n("split x 1"))
            act.wait_ge(adj_in, 16 * 2 * (1 + Q))
            copy(adjT_hi, adjT[:]).then_inc(w_hi_ready, 1)
            act.wait_ge(gate_w_in, 16 * 5)
            split_weight(0, "u3", raw["u3"])
            split_weight(1, "w4", sum4)
            split_q(n("q 1"))
            normalise(1, 0, 0)
            split_h0(0, 0)
            split_v(n("v 1"))
            take_S_aside(n("rel 1"))
            split_new(0, n("new first"))
            take_a_aside(0, feaA, n("adj first"))
            split_S(1)
            split_a(0, 0, feaA, n("adj first"))
            take_a_aside(1, tokA, n("adj' first"))
            split_a(0, 1, tokA, n("adj' first"))
            split_weight(2, "wz", sumz)
            act.wait_ge(bias_ready, 3)
            split_weight(3, "w5", sum5)
            split_weight(0, "u5", raw["u5"])
            reset_sigmoid(0)
            split_rh(0)
            normalise(1, 1, 1)
            split_h0(1, 1)
            update_sigmoid(0)
            split_new(1, n("new 0"))
            take_a_aside(0, feaA, n("adj 0"))
            split_a(1, 0, feaA, n("adj 0"))
            take_a_aside(1, tokA, n("adj' 0"))
            split_a(1, 1, tokA, n("adj' 0"))
            candidate_tanh(0)
            with act.Fori(0, PAIRS - 1) as i:
                for k in (1, 2, 3, 4, 5):
                    window(i, k, lambda name: use_in_round(name, i))
                window(i + 1, 0, lambda name: use_in_round(name, i))
            for k in (1, 2, 3, 4):
                window(PAIRS - 1, k, use_in_end, attention=False)
            window(PAIRS - 1, 5, use_in_end, attention=False, new=False)

        @block.vector
        def _(dve):
            def sub(dst, a, b):
                return nc.vector.tensor_tensor(dst, a, b, ALU.subtract)

            def tok_wait(n, b):
                dve.wait_ge(tok_full, 2 * n + (b + 1))

            def fea_wait(n, b):
                dve.wait_ge(fea_full, 2 * n + (b + 1))

            def split_weight(n, name, src):
                dve.wait_ge(w_hi_ready, n)
                sub(W_lo[name][:].rearrange("p c n -> p (c n)"), src,
                    W_hi[name][:].rearrange("p c n -> p (c n)")).then_inc(w_lo_ready, 1)

            def statistics(n, g, s, at):
                if n == 0:
                    dve.wait_ge(x_in[s], 16 * at)
                else:
                    dve.wait_ge(tok_taken, 2 * at + 2)
                for q in range(Q):
                    nc.vector.bn_stats(bn[n][:, q, :], x_s[s][:, q, :]).then_inc(bn_ready[n], 1)
                dve.wait_ge(bn_ready[n], Q * (g + 1))
                dve.wait_ge(fence_done[n], g)
                nc.vector.memset(fence[:, n:n + 1], 0.0).then_inc(fence_done[n], 1)
                for q in range(Q):
                    nc.vector.bn_aggr(mv[n][:, q, :], bn[n][:, q, :]).then_inc(mv_ready[n], 1)
                dve.wait_ge(mv_ready[n], Q * (g + 1))
                nc.vector.tensor_scalar(vare[n][:], mv[n][:, :, 1], EPS, None, ALU.add).then_inc(vare_ready[n], 1)

            def shifts(n, g):
                dve.wait_ge(rstd_ready[n], g + 1)
                nc.vector.scalar_tensor_tensor(shift[n][:], mv[n][:, :, 0], -1.0, rstd[n][:],
                                               ALU.mult, ALU.mult).then_inc(shift_ready[n], 1)

            def split_hx(g, n):
                for c in range(C):
                    tok_wait(n, c)
                    dve.wait_ge(hxT_hi_ready, 2 * g + (c + 1))
                    sub(hxT_lo[:, c, :], tokT[:, c, :], hxT_hi[:, c, :]).then_inc(tok_taken, 1)

            def split_q(g, n):
                for c in range(C):
                    fea_wait(n, c)
                    dve.wait_ge(q_hi_ready, 2 * g + (c + 1))
                    sub(q_lo[:, c, :], fea[:, c, :], q_hi[:, c, :]).then_inc(fea_taken, 1)

            def split_v(g, n):
                for b in range(2):
                    part = slice(HQ * b, HQ * b + HQ)
                    tok_wait(n, b)
                    dve.wait_ge(v_hi_ready, 2 * g + (b + 1))
                    sub(v_lo[:, part, :], tok[:, part, :], v_hi[:, part, :]).then_inc(tok_taken, 1)

            def mask_scores(g, n):
                fea_wait(n, 1)
                dve.wait_ge(S_aside_ready, g + 1)
                nc.vector.tensor_tensor(S_sum[:], feaA[:, :, 0, :], S_aside[:], ALU.add).then_inc(fea_taken, 2)
                dve.wait_ge(fea_taken, 2 * n + 2)
                nc.vector.tensor_tensor(S[:], S_sum[:], mask[:], ALU.mult).then_inc(S_ready, 1)

            def split_S(g):
                dve.wait_ge(S_hi_ready, g + 1)
                sub(S_lo[:], S[:], S_hi[:]).then_inc(S_lo_ready, 1)

            def take_norm(n):
                fea_wait(n, 1)
                nc.vector.tensor_copy(norm2[:], fea[:, 1, 0:Q]).then_inc(fea_taken, 2)

            def add_attention(g, s, n):
                dve.wait_ge(rnorm_ready, g + 1)
                for q in range(Q):
                    tok_wait(n, q // HQ)
                    last = nc.vector.scalar_tensor_tensor(x_s[s][:, q, :], tok[:, q, :], rnorm[:, q:q + 1],
                                                          x_s[s][:, q, :], ALU.mult, ALU.add)
                    if q % HQ == HQ - 1:
                        last.then_inc(tok_taken, 1)

            def split_state(w, o):
                for c in range(C):
                    dve.wait_ge(h_hi_ready, 2 * w + (c + 3))
                    sub(h_lo[o][:, c, :], h[o][:, c, :], h_hi[o][:, c, :]).then_inc(h_lo_ready, 1)

            def split_tok(v, n):
                for b in range(2):
                    part = slice(HQ * b, HQ * b + HQ)
                    tok_wait(n, b)
                    dve.wait_ge(t_hi_ready, 2 * v + (b + 1))
                    sub(t_lo[:, part, :], tok[:, part, :], t_hi[:, part, :]).then_inc(tok_taken, 1)

            def split_h0(v, s):
                for b in range(2):
                    part = slice(HQ * b, HQ * b + HQ)
                    dve.wait_ge(t_hi_ready, 2 * v + (b + 1))
                    sub(t_lo[:, part, :], h0[s][:, part, :], t_hi[:, part, :]).then_inc(t_lo_ready, 1)

            def sum_a(c, v, banks, n):
                wait, taken = (fea_wait, fea_taken) if banks is feaA else (tok_wait, tok_taken)
                wait(n, 1)
                dve.wait_ge(a_aside_ready, 2 * v + (c + 1))
                nc.vector.tensor_tensor(a_s[:, c, :].rearrange("p (q n) -> p q n", q=Q), banks[:, :, 0, :],
                                        a_aside[:, c, :].rearrange("p (q n) -> p q n", q=Q), ALU.add).then_inc(taken, 2)

            def split_a(v, s, c):
                dve.wait_ge(a_hi_ready, 2 * v + (c + 1))
                sub(a_lo[s][:, c, :], a_s[:, c, :], a_hi[s][:, c, :]).then_inc(a_lo_ready, 1)

            def take_new(v, s, n):
                for c in range(C):
                    dve.wait_ge(h_hi_ready, 2 * v + (c + 1))
                    nc.vector.tensor_copy(h[s][:, c, :], tokT[:, c, :]).then_inc(h_new_ready, 1)
                    sub(h_lo[s][:, c, :], tokT[:, c, :], h_hi[s][:, c, :]).then_inc(tok_taken, 1)

            def add_resid(g, s, n, stores):
                dve.wait_ge(resid_ready, g + 1)
                dve.wait_ge(stored[s], stores * 16 + 16)
                for b in range(2):
                    part = slice(HQ * b, HQ * b + HQ)
                    tok_wait(n, b)
                    nc.vector.tensor_tensor(o_s[s][:, part, :], tok[:, part, :], resid[s][:, part, :],
                                            ALU.add).then_inc(tok_taken, 1)

            def update(w, o):
                for c in range(C):
                    dve.wait_ge(c_ready, 2 * w + (c - 1))
                    sub(d_s[:, c, :], c_s[:, c, :], h[o][:, c, :]).then_inc(diff_ready, 1)
                for c in range(C):
                    dve.wait_ge(z_ready, 2 * w + (c - 1))
                    dve.wait_ge(diff_ready, 2 * w + (c - 1))
                    nc.vector.tensor_tensor(d_s[:, c, :], z_s[:, c, :], d_s[:, c, :], ALU.mult).then_inc(prod_ready, 1)
                for c in range(C):
                    dve.wait_ge(prod_ready, 2 * w + (c - 1))
                    nc.vector.tensor_tensor(h[o][:, c, :], h[o][:, c, :], d_s[:, c, :], ALU.add).then_inc(upd_ready, 1)

            def reset_state(w, s):
                for c in range(C):
                    dve.wait_ge(r_ready, 2 * w + (c + 1))
                    nc.vector.tensor_tensor(rh[:, c, :], r_s[:, c, :], h[s][:, c, :], ALU.mult).then_inc(rh_ready, 1)

            def split_rh(w):
                for c in range(C):
                    dve.wait_ge(rh_hi_ready, 2 * w + (c + 1))
                    sub(rh_lo[:, c, :], rh[:, c, :], rh_hi[:, c, :]).then_inc(rh_lo_ready, 1)

            def window(i, k, use, attention=True, new=True):
                w, s, o = 6 * i + k, k % 2, 1 - k % 2
                if k == 1:
                    update(w, o)
                    split_state(w, o)
                    dve.wait_ge(h_new_ready, 4 * i + 4)
                    reset_state(w, s)
                    split_tok(w + 1, use("step 1"))
                    if attention:
                        statistics(0, 2 * i + 2, 0, i + 2)
                    sum_a(0, w + 1, feaA, use("adj 1"))
                    if attention:
                        shifts(0, 2 * i + 2)
                    split_rh(w)
                    sum_a(1, w + 1, tokA, use("adj' 1"))
                    split_a(w + 1, o, 1)
                    split_a(w + 1, o, 0)
                    if attention:
                        split_hx(2 * i + 2, use("split x X"))
                elif k == 2:
                    update(w, o)
                    if attention:
                        split_q(2 * i + 2, use("q X"))
                    split_tok(w + 1, use("step 2"))
                    split_state(w, o)
                    reset_state(w, s)
                    sum_a(0, w + 1, feaA, use("adj 2"))
                    split_rh(w)
                    sum_a(1, w + 1, tokA, use("adj' 2"))
                    split_a(w + 1, o, 0)
                    if attention:
                        mask_scores(2 * i + 2, use("rel X"))
                        split_S(2 * i + 2)
                        statistics(0, 2 * i + 3, 1, i + 2)
                    split_a(w + 1, o, 1)
                    if attention:
                        split_v(2 * i + 2, use("v X"))
                elif k == 3:
                    if attention:
                        take_norm(use("norm X"))
                    update(w, o)
                    if attention:
                        shifts(0, 2 * i + 3)
                        add_attention(2 * i + 2, 0, use("sum X"))
                    split_state(w, o)
                    split_tok(w + 1, use("step 3"))
                    reset_state(w, s)
                    split_rh(w)
                    sum_a(0, w + 1, feaA, use("adj 3"))
                    sum_a(1, w + 1, tokA, use("adj' 3"))
                    if attention:
                        statistics(1, 2 * i + 2, 0, use("sum X"))
                    split_a(w + 1, o, 0)
                    split_a(w + 1, o, 1)
                    if attention:
                        split_hx(2 * i + 3, use("split x Y"))
                        shifts(1, 2 * i + 2)
                elif k == 4:
                    update(w, o)
                    if attention:
                        split_q(2 * i + 3, use("q Y"))
                    split_tok(w + 1, use("step 4"))
                    reset_state(w, s)
                    sum_a(0, w + 1, feaA, use("adj 4"))
                    split_rh(w)
                    sum_a(1, w + 1, tokA, use("adj' 4"))
                    split_state(w, o)
                    split_a(w + 1, o, 1)
                    if attention:
                        mask_scores(2 * i + 3, use("rel Y"))
                    split_a(w + 1, o, 0)
                    if attention:
                        split_S(2 * i + 3)
                        split_v(2 * i + 3, use("v Y"))
                elif k == 5:
                    update(w, o)
                    if attention:
                        take_norm(use("norm Y"))
                    if new:
                        split_h0(w + 1, o)
                    if attention:
                        add_attention(2 * i + 3, 1, use("sum Y"))
                    reset_state(w, s)
                    add_resid(2 * i, 0, use("final 5"), i)
                    if attention:
                        statistics(1, 2 * i + 3, 1, use("sum Y"))
                    if new:
                        take_new(w + 1, o, use("new 5"))
                    split_rh(w)
                    if new:
                        sum_a(0, w + 1, feaA, use("adj 5"))
                        sum_a(1, w + 1, tokA, use("adj' 5"))
                        split_a(w + 1, o, 0)
                    if attention:
                        shifts(1, 2 * i + 3)
                    if new:
                        split_a(w + 1, o, 1)
                else:
                    update(w, o)
                    split_h0(w + 1, o)
                    add_resid(2 * i - 1, 1, use("final 0"), i - 1)
                    dve.wait_ge(h_new_ready, 4 * i + 2)
                    reset_state(w, s)
                    split_rh(w)
                    take_new(w + 1, o, use("new 0"))
                    sum_a(0, w + 1, feaA, use("adj 0"))
                    sum_a(1, w + 1, tokA, use("adj' 0"))
                    split_a(w + 1, o, 0)
                    split_a(w + 1, o, 1)

            n = use_in_start
            statistics(0, 0, 0, 1)
            shifts(0, 0)
            dve.wait_ge(m_full, 1)
            split_weight(1, "m", gate[:, 0, :])
            split_hx(0, n("split x 0"))
            split_weight(2, "v", raw["v"])
            statistics(0, 1, 1, 1)
            shifts(0, 1)
            split_q(0, n("q 0"))
            split_v(0, n("v 0"))
            dve.wait_ge(adj_in, 16 * 2 * (1 + Q))
            mask_scores(0, n("rel 0"))
            split_S(0)
            split_hx(1, n("split x 1"))
            dve.wait_ge(w_hi_ready, 3)
            sub(adjT_lo, adjT[:], adjT_hi).then_inc(w_lo_ready, 1)
            take_norm(n("norm 0"))
            dve.wait_ge(gate_w_in, 16 * 5)
            nc.vector.tensor_tensor(sum4, raw["w4"][:, 0, :], raw["w4"][:, 1, :], ALU.add).then_inc(w_sum, 1)
            add_attention(0, 0, n("sum 0"))
            statistics(1, 0, 0, n("sum 0"))
            split_weight(4, "u3", raw["u3"])
            shifts(1, 0)
            split_q(1, n("q 1"))
            split_weight(5, "w4", sum4)
            nc.vector.tensor_tensor(sumz, raw["w3"][:, 0, :], raw["w3"][:, 1, :], ALU.add).then_inc(sum3_ready, 1)
            dve.wait_ge(w_sum, 1)
            dve.wait_ge(sum3_ready, 1)
            sub(sumz, sumz, sum4).then_inc(w_sum, 1)
            split_h0(0, 0)
            split_v(1, n("v 1"))
            mask_scores(1, n("rel 1"))
            take_new(0, 0, n("new first"))
            sum_a(0, 0, feaA, n("adj first"))
            split_S(1)
            split_a(0, 0, 0)
            sum_a(1, 0, tokA, n("adj' first"))
            split_a(0, 0, 1)
            nc.vector.tensor_tensor(sum5, raw["w5"][:, 0, :], raw["w5"][:, 1, :], ALU.add).then_inc(w_sum, 1)
            dve.wait_ge(bias_in, 16 * 5)
            for dst, (m1, m2) in ((b_r, (2, 1)), (b_z, (0, 1)), (b_c, (3, 4))):
                nc.vector.tensor_tensor(dst[:], b_in[:, m1, :], b_in[:, m2, :], ALU.add).then_inc(bias_ready, 1)
            split_weight(6, "wz", sumz)
            take_norm(n("norm 1"))
            split_weight(7, "w5", sum5)
            add_attention(1, 1, n("sum 1"))
            statistics(1, 1, 1, n("sum 1"))
            split_weight(8, "u5", raw["u5"])
            dve.wait_ge(w_lo_ready, len(names) + 1)
            dve.wait_ge(h_new_ready, 2)
            reset_state(0, 0)
            shifts(1, 1)
            split_rh(0)
            split_h0(1, 1)
            take_new(1, 1, n("new 0"))
            sum_a(0, 1, feaA, n("adj 0"))
            sum_a(1, 1, tokA, n("adj' 0"))
            split_a(1, 1, 0)
            split_a(1, 1, 1)
            with dve.Fori(0, PAIRS - 1) as i:
                for k in (1, 2, 3, 4, 5):
                    window(i, k, lambda name: use_in_round(name, i))
                window(i + 1, 0, lambda name: use_in_round(name, i))
            for k in (1, 2, 3, 4):
                window(PAIRS - 1, k, use_in_end, attention=False)
            window(PAIRS - 1, 5, use_in_end, attention=False, new=False)
            update(6 * PAIRS, 1)
            add_resid(G - 1, 1, use_in_end("final 0"), PAIRS - 1)


def kernel(x, adj, L0_gnn_Wq, L0_gnn_Wk, L0_gnn_Wv, L1_gnn_w3_w, L1_gnn_w3_b, L1_gnn_u3_w, L1_gnn_u3_b,
           L1_gnn_w4_w, L1_gnn_w4_b, L1_gnn_w5_w, L1_gnn_w5_b, L1_gnn_u5_w, L1_gnn_u5_b):
    import numpy as np
    import concourse.bacc as bacc
    from concourse import mybir
    from concourse.bass_utils import run_bass_kernel_spmd

    def turned(a):
        return np.ascontiguousarray(np.asarray(a).T)

    def column(a):
        return np.ascontiguousarray(np.asarray(a).reshape(-1, 128).T)

    arrays = {
        "x": np.ascontiguousarray(x), "adj": np.ascontiguousarray(adj), "adj_t": turned(adj),
        "wq": np.ascontiguousarray(L0_gnn_Wq), "wk": np.ascontiguousarray(L0_gnn_Wk), "wv_t": turned(L0_gnn_Wv),
        "w3_t": turned(L1_gnn_w3_w), "b3": column(L1_gnn_w3_b), "u3_t": turned(L1_gnn_u3_w), "bu3": column(L1_gnn_u3_b),
        "w4_t": turned(L1_gnn_w4_w), "b4": column(L1_gnn_w4_b), "w5_t": turned(L1_gnn_w5_w), "b5": column(L1_gnn_w5_b),
        "u5_t": turned(L1_gnn_u5_w), "bu5": column(L1_gnn_u5_b),
    }
    nc = bacc.Bacc("TRN2", target_bir_lowering=False, num_devices=1)
    args = {n: nc.dram_tensor(n, a.shape, mybir.dt.from_np(a.dtype), kind="ExternalInput").ap()
            for n, a in arrays.items()}
    out = nc.dram_tensor("out", x.shape, mybir.dt.float32, kind="ExternalOutput").ap()
    gated_graph_kernel(nc, *args.values(), out)
    r = run_bass_kernel_spmd(nc, [arrays], core_ids=[0])
    return r.results[0]["out"]
```
